# Optimizing a Trainium2 kernel written in Bass

```python
import numpy as np
import jax
import jax.numpy as jnp

def _softmax(x, axis=-1):
    return jax.nn.softmax(x, axis=axis)
def _gelu(x):
    return jax.nn.gelu(x, approximate=True)
def _silu(x):
    return jax.nn.silu(x)
def _sigmoid(x):
    return jax.nn.sigmoid(x)
def _layernorm(x, axis=-1, eps=1e-5):
    m = jnp.mean(x, axis=axis, keepdims=True)
    v = jnp.var(x, axis=axis, keepdims=True)
    return (x - m) / jnp.sqrt(v + eps)
def _scatter_add(tgt, idx, src, axis=0):
    return tgt.at[idx].add(src)
def _segment_sum(src, seg, n):
    return jax.ops.segment_sum(src, seg, n)

kernel_name = 'mk_conv_preact_d2_conv_nchw512_d53f94'

def setup_inputs(seed: int = 0):
    np.random.seed(seed)
    _w = jnp.asarray
    def _rec_inputs():
        import jax
        import jax.numpy as jnp
        _gk = jax.random.key(seed)
        x = -0.0002928 + 1 * jax.random.normal(jax.random.fold_in(_gk, 1), (2, 512, 64, 64), jnp.float32)
        return x
    x = _rec_inputs()
    def _L0_conv_setup():
        import jax, jax.numpy as jnp
        import numpy as np
        DIM = 512
        D_STATE = 16
        D_CONV = 4
        D_INNER = 1024
        DT_RANK = 32
        EPS = 1e-05

        def _selective_scan(u, delta, A, Bm, Cm, D_skip):

            def step(h, inp):
                u_t, d_t, b_t, c_t = inp
                dA = jnp.exp(d_t[..., None] * A)
                dBu = (d_t * u_t)[..., None] * b_t[:, None, :]
                h = dA * h + dBu
                y = jnp.einsum('bdn,bn->bd', h, c_t)
                return (h, y)
            B, L, d = u.shape
            h0 = jnp.zeros((B, d, A.shape[1]), u.dtype)
            xs = (u.transpose(1, 0, 2), delta.transpose(1, 0, 2), Bm.transpose(1, 0, 2), Cm.transpose(1, 0, 2))
            _, ys = jax.lax.scan(step, h0, xs)
            y = ys.transpose(1, 0, 2)
            return y + u * D_skip

        def _mamba_layer(x, ln_w, ln_b, in_proj_w, conv_w, conv_b, x_proj_w, dt_proj_w, dt_proj_b, A_log, D_skip, out_proj_w):
            B, C = x.shape[:2]
            img_dims = x.shape[2:]
            xf = x.reshape(B, C, -1).transpose(0, 2, 1)
            mu = jnp.mean(xf, -1, keepdims=True)
            var = jnp.mean(jnp.square(xf - mu), -1, keepdims=True)
            xn = (xf - mu) * jax.lax.rsqrt(var + EPS) * ln_w + ln_b
            xz = xn @ in_proj_w.T
            xin, z = jnp.split(xz, 2, axis=-1)
            xc = xin.transpose(0, 2, 1)
            w = conv_w[:, None, :]
            xc = jax.lax.conv_general_dilated(xc, w, window_strides=(1,), padding=[(D_CONV - 1, 0)], feature_group_count=D_INNER, dimension_numbers=('NCH', 'OIH', 'NCH'))
            xc = jax.nn.silu(xc + conv_b[None, :, None])
            xs = xc.transpose(0, 2, 1)
            x_dbl = xs @ x_proj_w.T
            dt = x_dbl[..., :DT_RANK]
            Bm = x_dbl[..., DT_RANK:DT_RANK + D_STATE]
            Cm = x_dbl[..., DT_RANK + D_STATE:]
            delta = jax.nn.softplus(dt @ dt_proj_w.T + dt_proj_b)
            A = -jnp.exp(A_log)
            y = _selective_scan(xs, delta, A, Bm, Cm, D_skip)
            y = y * jax.nn.silu(z)
            out = y @ out_proj_w.T
            return out.transpose(0, 2, 1).reshape(B, C, *img_dims)
        key = jax.random.key(seed)
        ks = jax.random.split(key, 8)
        s = 0.02
        x = jax.random.normal(ks[0], (2, DIM, 64, 64), jnp.float32)
        in_proj_w = jax.random.normal(ks[1], (2 * D_INNER, DIM), jnp.float32) * s
        conv_w = jax.random.normal(ks[2], (D_INNER, D_CONV), jnp.float32) * 0.25
        conv_b = jnp.zeros((D_INNER,), jnp.float32)
        x_proj_w = jax.random.normal(ks[3], (DT_RANK + 2 * D_STATE, D_INNER), jnp.float32) * s
        dt_proj_w = jax.random.normal(ks[4], (D_INNER, DT_RANK), jnp.float32) * DT_RANK ** (-0.5)
        dt_proj_b = jnp.full((D_INNER,), -4.0, jnp.float32)
        A_log = jnp.log(jnp.broadcast_to(jnp.arange(1, D_STATE + 1, dtype=jnp.float32), (D_INNER, D_STATE)))
        D_skip = jnp.ones((D_INNER,), jnp.float32)
        out_proj_w = jax.random.normal(ks[5], (DIM, D_INNER), jnp.float32) * s
        ln_w = jnp.ones((DIM,), jnp.float32)
        ln_b = jnp.zeros((DIM,), jnp.float32)
        return {'x': x, 'ln_w': ln_w, 'ln_b': ln_b, 'in_proj_w': in_proj_w, 'conv_w': conv_w, 'conv_b': conv_b, 'x_proj_w': x_proj_w, 'dt_proj_w': dt_proj_w, 'dt_proj_b': dt_proj_b, 'A_log': A_log, 'D_skip': D_skip, 'out_proj_w': out_proj_w}
    _L0_conv_all = _L0_conv_setup()
    _L0_conv_in = {k: v for k, v in _L0_conv_all.items() if k in ('ln_w', 'ln_b', 'in_proj_w', 'conv_w', 'conv_b', 'x_proj_w', 'dt_proj_w', 'dt_proj_b', 'A_log', 'D_skip', 'out_proj_w', )}
    del _L0_conv_all

    def _L1_conv_setup():
        import jax, jax.numpy as jnp
        import numpy as np
        DIM = 512
        HEADS = 8
        DIM_HEAD = 64
        HIDDEN = HEADS * DIM_HEAD
        B, H, W = (16, 64, 64)
        key = jax.random.key(seed)
        k1, k2, k3, k4 = jax.random.split(key, 4)
        x = jax.random.normal(k1, (B, DIM, H, W), dtype=jnp.float32)
        w_qkv = jax.random.normal(k2, (3 * HIDDEN, DIM), dtype=jnp.float32) * (1.0 / np.sqrt(DIM))
        w_out = jax.random.normal(k3, (DIM, HIDDEN), dtype=jnp.float32) * (1.0 / np.sqrt(HIDDEN))
        b_out = jax.random.normal(k4, (DIM,), dtype=jnp.float32) * 0.01
        return {'x': x, 'w_qkv': w_qkv, 'w_out': w_out, 'b_out': b_out}
    _L1_conv_all = _L1_conv_setup()
    _L1_conv_in = {k: v for k, v in _L1_conv_all.items() if k in ('w_qkv', 'w_out', 'b_out', )}
    del _L1_conv_all

    return {
        "x": x,
        "L0_conv_ln_w": _L0_conv_in["ln_w"],
        "L0_conv_ln_b": _L0_conv_in["ln_b"],
        "L0_conv_in_proj_w": _L0_conv_in["in_proj_w"],
        "L0_conv_conv_w": _L0_conv_in["conv_w"],
        "L0_conv_conv_b": _L0_conv_in["conv_b"],
        "L0_conv_x_proj_w": _L0_conv_in["x_proj_w"],
        "L0_conv_dt_proj_w": _L0_conv_in["dt_proj_w"],
        "L0_conv_dt_proj_b": _L0_conv_in["dt_proj_b"],
        "L0_conv_A_log": _L0_conv_in["A_log"],
        "L0_conv_D_skip": _L0_conv_in["D_skip"],
        "L0_conv_out_proj_w": _L0_conv_in["out_proj_w"],
        "L1_conv_w_qkv": _L1_conv_in["w_qkv"],
        "L1_conv_w_out": _L1_conv_in["w_out"],
        "L1_conv_b_out": _L1_conv_in["b_out"],
    }

def reference(x, L0_conv_ln_w, L0_conv_ln_b, L0_conv_in_proj_w, L0_conv_conv_w, L0_conv_conv_b, L0_conv_x_proj_w, L0_conv_dt_proj_w, L0_conv_dt_proj_b, L0_conv_A_log, L0_conv_D_skip, L0_conv_out_proj_w, L1_conv_w_qkv, L1_conv_w_out, L1_conv_b_out):
    import jax
    import jax.numpy as jnp
    def _L0_conv_ref(x, ln_w, ln_b, in_proj_w, conv_w, conv_b, x_proj_w, dt_proj_w, dt_proj_b, A_log, D_skip, out_proj_w):
        import jax, jax.numpy as jnp
        import numpy as np
        DIM = 512
        D_STATE = 16
        D_CONV = 4
        D_INNER = 1024
        DT_RANK = 32
        EPS = 1e-05

        def _selective_scan(u, delta, A, Bm, Cm, D_skip):

            def step(h, inp):
                u_t, d_t, b_t, c_t = inp
                dA = jnp.exp(d_t[..., None] * A)
                dBu = (d_t * u_t)[..., None] * b_t[:, None, :]
                h = dA * h + dBu
                y = jnp.einsum('bdn,bn->bd', h, c_t)
                return (h, y)
            B, L, d = u.shape
            h0 = jnp.zeros((B, d, A.shape[1]), u.dtype)
            xs = (u.transpose(1, 0, 2), delta.transpose(1, 0, 2), Bm.transpose(1, 0, 2), Cm.transpose(1, 0, 2))
            _, ys = jax.lax.scan(step, h0, xs)
            y = ys.transpose(1, 0, 2)
            return y + u * D_skip

        def _mamba_layer(x, ln_w, ln_b, in_proj_w, conv_w, conv_b, x_proj_w, dt_proj_w, dt_proj_b, A_log, D_skip, out_proj_w):
            B, C = x.shape[:2]
            img_dims = x.shape[2:]
            xf = x.reshape(B, C, -1).transpose(0, 2, 1)
            mu = jnp.mean(xf, -1, keepdims=True)
            var = jnp.mean(jnp.square(xf - mu), -1, keepdims=True)
            xn = (xf - mu) * jax.lax.rsqrt(var + EPS) * ln_w + ln_b
            xz = xn @ in_proj_w.T
            xin, z = jnp.split(xz, 2, axis=-1)
            xc = xin.transpose(0, 2, 1)
            w = conv_w[:, None, :]
            xc = jax.lax.conv_general_dilated(xc, w, window_strides=(1,), padding=[(D_CONV - 1, 0)], feature_group_count=D_INNER, dimension_numbers=('NCH', 'OIH', 'NCH'))
            xc = jax.nn.silu(xc + conv_b[None, :, None])
            xs = xc.transpose(0, 2, 1)
            x_dbl = xs @ x_proj_w.T
            dt = x_dbl[..., :DT_RANK]
            Bm = x_dbl[..., DT_RANK:DT_RANK + D_STATE]
            Cm = x_dbl[..., DT_RANK + D_STATE:]
            delta = jax.nn.softplus(dt @ dt_proj_w.T + dt_proj_b)
            A = -jnp.exp(A_log)
            y = _selective_scan(xs, delta, A, Bm, Cm, D_skip)
            y = y * jax.nn.silu(z)
            out = y @ out_proj_w.T
            return out.transpose(0, 2, 1).reshape(B, C, *img_dims)
        return _mamba_layer(x, ln_w, ln_b, in_proj_w, conv_w, conv_b, x_proj_w, dt_proj_w, dt_proj_b, A_log, D_skip, out_proj_w)

    def _L1_conv_ref(x, w_qkv, w_out, b_out):
        import jax, jax.numpy as jnp
        import numpy as np
        DIM = 512
        HEADS = 8
        DIM_HEAD = 64
        HIDDEN = HEADS * DIM_HEAD
        B, H, W = (16, 64, 64)
        b, c, h, w = x.shape
        l = h * w
        xf = x.reshape(b, c, l)
        qkv = jnp.einsum('oc,bcl->bol', w_qkv, xf)
        q, k, v = jnp.split(qkv, 3, axis=1)
        q = q.reshape(b, HEADS, DIM_HEAD, l)
        k = jax.nn.softmax(k.reshape(b, HEADS, DIM_HEAD, l), axis=-1)
        v = v.reshape(b, HEADS, DIM_HEAD, l)
        context = jnp.einsum('bhdl,bhel->bhde', k, v)
        out = jnp.einsum('bhde,bhdl->bhel', context, q)
        out = out.reshape(b, HIDDEN, l)
        y = jnp.einsum('oc,bcl->bol', w_out, out) + b_out[None, :, None]
        return y.reshape(b, c, h, w)

    def _gn(v, G=32, eps=1e-5):
        B_, C_, H_, W_ = v.shape
        g = v.reshape(B_, G, C_ // G, H_, W_)
        m = jnp.mean(g, axis=(2, 3, 4), keepdims=True)
        s = jnp.var(g, axis=(2, 3, 4), keepdims=True)
        return ((g - m) / jnp.sqrt(s + eps)).reshape(v.shape)

    def _ln_c(v, eps=1e-6):
        m = jnp.mean(v, axis=1, keepdims=True)
        s = jnp.var(v, axis=1, keepdims=True)
        return (v - m) / jnp.sqrt(s + eps)

    def _ln_t(v, eps=1e-5):
        m = jnp.mean(v, axis=-1, keepdims=True)
        s = jnp.var(v, axis=-1, keepdims=True)
        return (v - m) / jnp.sqrt(s + eps)

    def _to_tokens(v):
        B_, C_, H_, W_ = v.shape
        return v.reshape(B_, C_, H_ * W_).transpose(0, 2, 1)
    def _from_tokens(t, like):
        B_, C_, H_, W_ = like.shape
        return t.transpose(0, 2, 1).reshape(B_, C_, H_, W_)

    x = x + _L0_conv_ref(_gn(x), L0_conv_ln_w, L0_conv_ln_b, L0_conv_in_proj_w, L0_conv_conv_w, L0_conv_conv_b, L0_conv_x_proj_w, L0_conv_dt_proj_w, L0_conv_dt_proj_b, L0_conv_A_log, L0_conv_D_skip, L0_conv_out_proj_w)
    x = x + _L1_conv_ref(_gn(x), L1_conv_w_qkv, L1_conv_w_out, L1_conv_b_out)
    return x


_drawn_inputs = setup_inputs


def setup_inputs(seed=0):
    import zlib

    import numpy as np

    out = dict(_drawn_inputs(seed))
    spreads = {'L0_conv_ln_w': (1.0, 0.6),
     'L0_conv_ln_b': (0.0, 0.8),
     'L0_conv_conv_b': (0.0, 0.458),
     'L0_conv_dt_proj_b': (-4.0, 0.6),
     'L0_conv_D_skip': (1.0, 0.6)}
    factors = {'L0_conv_x_proj_w': 8.0,
     'L0_conv_dt_proj_w': 8.0,
     'L0_conv_A_log': 8.0,
     'L1_conv_b_out': 52.056}
    for name, (base, spread) in spreads.items():
        noise = np.random.default_rng([zlib.crc32(name.encode()), seed]).standard_normal(out[name].shape)
        drawn = base * np.exp(spread * noise) if base else spread * noise
        out[name] = jnp.asarray(drawn.astype(out[name].dtype))
    for name, factor in factors.items():
        out[name] = (out[name] * factor).astype(out[name].dtype)
    return out
```

```python
import concourse.bass as bass
from concourse import mybir
from concourse.alu_op_type import AluOpType
from contextlib import ExitStack

FP32 = mybir.dt.float32
ALU = mybir.AluOpType
ACT = mybir.ActivationFunctionType
AX = mybir.AxisListType

P = 128
BATCH, DIM, TOKENS = 2, 512, 4096
CT = DIM // P
T = 512
CB = TOKENS // T
CHUNKS = BATCH * CB
INNER, STATE, TAPS, RANK = 1024, 16, 4, 32
JT = INNER // P
STEPS = JT * STATE
GROUP = DIM // 32
LN_EPS = 1e-5
GN_EPS = 1e-5
H_RING, HC_RING, DA_RING = 4, 2, 2


def wait(engine, sem, value):
    if isinstance(value, int) and value <= 0:
        return
    engine.wait_ge(sem, value)


def group_coefficients(nc, ctx, block, name, stats, tiles, per_tile, averages, psum, scale, bias):
    mv = ctx.enter_context(nc.sbuf_tensor(f"{name}_mean_var", [P, tiles, 2], FP32))
    gm = ctx.enter_context(nc.sbuf_tensor(f"{name}_group_mean", [P, tiles], FP32))
    dev = ctx.enter_context(nc.sbuf_tensor(f"{name}_spread", [P, tiles], FP32))
    gv = ctx.enter_context(nc.sbuf_tensor(f"{name}_group_var", [P, tiles], FP32))
    tmp = ctx.enter_context(nc.sbuf_tensor(f"{name}_tmp", [P, tiles], FP32))
    v_step = ctx.enter_context(nc.semaphore(f"{name}_v_step"))
    mean_mm = ctx.enter_context(nc.semaphore(f"{name}_mean_mm"))
    var_mm = ctx.enter_context(nc.semaphore(f"{name}_var_mm"))
    a_step = ctx.enter_context(nc.semaphore(f"{name}_a_step"))
    mean_ps, var_ps = psum[:, 0:tiles], psum[:, 64:64 + tiles]

    def vector(dve, done):
        count = [0]

        def step(instruction):
            count[0] += 1
            instruction.then_inc(v_step, 1)
            dve.wait_ge(v_step, count[0])

        for i in range(tiles):
            last = dve.bn_aggr(mv[:, i, :], stats(i))
            if i < tiles - 1:
                last.then_inc(v_step, 1)
                count[0] += 1
        step(last)
        dve.wait_ge(mean_mm, 1)
        step(dve.tensor_copy(gm[:, :], mean_ps))
        step(dve.tensor_tensor(dev[:, :], mv[:, :, 0], gm[:, :], ALU.subtract))
        step(dve.tensor_tensor(dev[:, :], dev[:, :], dev[:, :], ALU.mult))
        step(dve.tensor_tensor(dev[:, :], dev[:, :], mv[:, :, 1], ALU.add))
        dve.wait_ge(var_mm, 1)
        step(dve.tensor_scalar(gv[:, :], var_ps, GN_EPS, None, ALU.add))
        dve.wait_ge(a_step, 2)
        step(dve.tensor_tensor(tmp[:, :], scale, scale, ALU.mult))
        step(dve.tensor_tensor(tmp[:, :], tmp[:, :], gv[:, :], ALU.mult))
        step(dve.tensor_scalar(tmp[:, :], tmp[:, :], -0.5, 1.5, ALU.mult, ALU.add))
        step(dve.tensor_tensor(scale, scale, tmp[:, :], ALU.mult))
        dve.scalar_tensor_tensor(bias, gm[:, :], -1.0, scale, ALU.mult, ALU.mult).then_inc(done, 1)

    def tensor(pe):
        pe.wait_ge(v_step, tiles)
        pe.matmul(mean_ps, averages, mv[:, :, 0], start=True, stop=True).then_inc(mean_mm, 1)
        pe.wait_ge(v_step, tiles + 4)
        pe.matmul(var_ps, averages, dev[:, :], start=True, stop=True).then_inc(var_mm, 1)

    def scalar(act):
        act.wait_ge(v_step, tiles + 5)
        act.activation(scale, gv[:, :], ACT.Ln).then_inc(a_step, 1)
        act.wait_ge(a_step, 1)
        act.activation(scale, scale, ACT.Exp, scale=-0.5).then_inc(a_step, 1)

    return vector, tensor, scalar


def mamba_and_linear_attention(nc, x, ln_w, ln_b, in_proj, conv_w, conv_b, x_proj, dt_proj, dt_b, a_log, d_skip,
                               out_proj, qkv, q_rows, w_out1, b_out1, out):
    x_v = x.rearrange("b (ct p) (cb t) -> b cb p ct t", p=P, t=T)
    x2_d = nc.dram_tensor("x2", [BATCH, DIM, TOKENS], FP32).ap()
    x2_v = x2_d.rearrange("b (ct p) (cb t) -> b cb ct p t", p=P, t=T)
    x_tile_v = x.rearrange("b (ct p) (cb t) -> b cb ct p t", p=P, t=T)
    bc_d = nc.dram_tensor("b_and_c_rows", [2 * STATE, T], FP32).ap()

    outer = ExitStack()
    with outer:
        def sb(name, shape, stack=outer):
            return stack.enter_context(nc.sbuf_tensor(name, shape, FP32))

        def sem(name):
            return outer.enter_context(nc.semaphore(name))

        identity = sb("identity", [P, P])
        averages = sb("averages", [P, P])
        x2_stats = sb("x2_stats", [P, CT, CHUNKS, 6])

        layer0 = ExitStack()
        with layer0:
            w_in = sb("w_in", [P, CT, 2 * INNER], layer0)
            w_out = sb("w_out", [P, JT, DIM], layer0)
            w_x = sb("w_x", [P, JT, 64], layer0)
            w_dt = sb("w_dt", [RANK, INNER], layer0)
            w_conv = sb("w_conv", [P, JT, TAPS], layer0)
            b_conv = sb("b_conv", [P, JT], layer0)
            b_dt = sb("b_dt", [P, JT], layer0)
            skip = sb("skip", [P, JT], layer0)
            w_ln = sb("w_ln", [P, CT], layer0)
            b_ln = sb("b_ln", [P, CT], layer0)
            neg_a = sb("neg_a", [P, JT, STATE], layer0)
            channel_mean = sb("channel_mean", [P, P], layer0)
            eps = sb("eps", [P, 1], layer0)
            keep_now = sb("keep_now", [P, 2], layer0)
            one = sb("one", [P, 1], layer0)
            keep = sb("keep", [P, CHUNKS + 2], layer0)
            gn_scale = sb("gn_scale", [P, BATCH * CT], layer0)
            gn_bias = sb("gn_bias", [P, BATCH * CT], layer0)

            bc = sb("bc", [P, 2, STATE, T], layer0)
            xs = sb("xs", [P, 2, JT, T], layer0)
            xn = sb("xn", [P, 2, CT, T], layer0)
            sq = sb("sq", [P, 2, T], layer0)
            acc = sb("acc", [P, T], layer0)
            zs = sb("zs", [P, T], layer0)
            halo = sb("halo", [P, JT, TAPS - 1], layer0)
            carry = sb("carry", [P, STEPS], layer0)
            sp_e = sb("sp_e", [P, T], layer0)
            sp_w = sb("sp_w", [P, T], layer0)
            sp_m = sb("sp_m", [P, T], layer0)
            delta = sb("delta", [P, 2, T], layer0)
            hs = sb("hs", [P, H_RING, T], layer0)
            hc = sb("hc", [P, HC_RING, T], layer0)
            xres = sb("xres", [P, 2, T], layer0)
            dbl = sb("dbl", [64, T], layer0)

            banks = [layer0.enter_context(nc.psum_tensor(f"bank{i}", [P, T], FP32)) for i in range(8)]
            y_ps, da_ps = banks[0:2], banks[2:4]
            du_ps, pa, pb, pout = banks[4:8]

            weights_in = sem("weights_in")
            xin_stage = [sem(f"x_stage{i}") for i in range(2)]
            stats_done = sem("stats_done")
            consts = sem("consts")
            halved = sem("halved")
            a_exp = sem("a_exp")
            gn_done = sem("gn_done")
            n_weights = 11

            with ExitStack() as setup:
                stage = bc[:, :, :, :].rearrange("p a n t -> p a (n t)")
                first_stats = sq[:, :, :].rearrange("p a t -> p (a t)")[:, 0:BATCH * CT * CB * 6]
                first_stats = first_stats.rearrange("p (i s) -> p i s", i=BATCH * CT)
                block = setup.enter_context(nc.Block())
                gc_vector, gc_tensor, gc_scalar = group_coefficients(
                    nc, setup, block, "gn0", lambda i: first_stats[:, i, :], BATCH * CT, CB, averages[:, :], pa,
                    gn_scale[:, :], gn_bias[:, :])

                @block.sync
                def _(sp):
                    x_rows = x.rearrange("b (ct p) l -> (b ct) p l", p=P)
                    for i in range(BATCH * CT):
                        wait(sp, stats_done, CB * (i - 1))
                        sp.dma_start(stage[:, i % 2, 0:TOKENS], x_rows[i]).then_inc(xin_stage[i % 2], 16)
                    sp.dma_start(w_in[:, :, :], in_proj.rearrange("(ct p) n -> p ct n", p=P)).then_inc(weights_in, 16)
                    sp.dma_start(w_out[:, :, :], out_proj.rearrange("(j p) n -> p j n", p=P)).then_inc(weights_in, 16)
                    sp.dma_start(w_x[:, :, :], x_proj.rearrange("(j p) n -> p j n", p=P)).then_inc(weights_in, 16)
                    sp.dma_start(w_dt[:, :], dt_proj).then_inc(weights_in, 16)
                    sp.dma_start(w_conv[:, :, :], conv_w).then_inc(weights_in, 16)
                    sp.dma_start(b_conv[:, :], conv_b).then_inc(weights_in, 16)
                    sp.dma_start(b_dt[:, :], dt_b).then_inc(weights_in, 16)
                    sp.dma_start(skip[:, :], d_skip).then_inc(weights_in, 16)
                    sp.dma_start(w_ln[:, :], ln_w).then_inc(weights_in, 16)
                    sp.dma_start(b_ln[:, :], ln_b).then_inc(weights_in, 16)
                    sp.dma_start(neg_a[:, :, :], a_log).then_inc(weights_in, 16)
                    sp.wait_ge(weights_in, 16 * n_weights)

                @block.gpsimd
                def _(pool):
                    pool.memset(identity[:, :], 1.0).then_inc(consts, 1)
                    pool.memset(averages[:, :], 1.0 / GROUP).then_inc(consts, 1)
                    pool.memset(channel_mean[:, :], 1.0 / DIM).then_inc(consts, 1)
                    pool.memset(keep[:, :], 1.0).then_inc(consts, 1)
                    pool.memset(halo[:, :, :], 0.0).then_inc(consts, 1)
                    pool.memset(carry[:, :], 0.0).then_inc(consts, 1)
                    pool.memset(eps[:, :], LN_EPS).then_inc(consts, 1)
                    pool.memset(one[:, :], 1.0).then_inc(consts, 1)
                    pool.wait_ge(consts, 8)
                    pool.affine_select(out=identity[:, :], in_=identity[:, :], compare_op=ALU.is_equal, fill=0.0,
                                       base=0, pattern=[[-1, P]], channel_multiplier=1).then_inc(consts, 1)
                    groups = averages[:, :].rearrange("p (a g) -> p a g", g=GROUP)
                    pool.affine_select(out=groups, in_=groups, compare_op=ALU.is_ge, fill=0.0, base=0,
                                       pattern=[[-GROUP, P // GROUP], [0, GROUP]],
                                       channel_multiplier=1).then_inc(consts, 1)
                    pool.memset(keep[:, CB:CB + 1], 0.0).then_inc(consts, 1)
                    pool.wait_ge(consts, 11)
                    pool.affine_select(out=groups, in_=groups, compare_op=ALU.is_ge, fill=0.0, base=GROUP - 1,
                                       pattern=[[GROUP, P // GROUP], [0, GROUP]],
                                       channel_multiplier=-1).then_inc(consts, 1)
                    pool.wait_ge(weights_in, 16 * n_weights)
                    pool.tensor_scalar(w_in[:, :, INNER:], w_in[:, :, INNER:], 0.5, None, ALU.mult).then_inc(halved, 1)
                    pool.tensor_scalar(w_conv[:, :, :], w_conv[:, :, :], 0.5, None, ALU.mult).then_inc(halved, 1)
                    pool.tensor_scalar(b_conv[:, :], b_conv[:, :], 0.5, None, ALU.mult).then_inc(halved, 1)
                    pool.wait_ge(a_exp, 1)
                    pool.tensor_scalar(neg_a[:, :, :], neg_a[:, :, :], -1.0, None, ALU.mult).then_inc(halved, 1)

                @block.vector
                def _(dve):
                    for i in range(BATCH * CT):
                        dve.wait_ge(xin_stage[i % 2], 16 * (i // 2 + 1))
                        for k in range(CB):
                            dve.bn_stats(first_stats[:, i, 6 * k:6 * k + 6],
                                         stage[:, i % 2, k * T:(k + 1) * T]).then_inc(stats_done, 1)
                    dve.wait_ge(stats_done, BATCH * CT * CB)
                    gc_vector(dve, gn_done)

                @block.tensor
                def _(pe):
                    pe.wait_ge(consts, 12)
                    gc_tensor(pe)

                @block.scalar
                def _(act):
                    act.wait_ge(weights_in, 16 * n_weights)
                    act.activation(neg_a[:, :, :], neg_a[:, :, :], ACT.Exp).then_inc(a_exp, 1)
                    gc_scalar(act)

            sp_fence, act_fence = sem("sp_fence"), sem("act_fence")
            keep_set, carried = sem("keep_set"), sem("carried")
            x_loaded = sem("x_loaded")
            gn_applied = sem("gn_applied")
            mean_mm = sem("mean_mm")
            centered = sem("centered")
            squared = sem("squared")
            var_mm = sem("var_mm")
            rstd_guess = sem("rstd_guess")
            newton = sem("newton")
            scaled = sem("scaled")
            xn_ready = sem("xn_ready")
            in_mm = sem("in_mm")
            tap3 = sem("tap3")
            conv_step = sem("conv_step")
            halo_saved = sem("halo_saved")
            tanh_x = sem("tanh_x")
            xs_ready = sem("xs_ready")
            x_mm = sem("x_mm")
            dbl_ready = sem("dbl_ready")
            bc_stored = sem("bc_stored")
            bc_loaded = [sem(f"bc_loaded{n}") for n in range(STATE)]
            dt_mm = sem("dt_mm")
            dt_read = sem("dt_read")
            sp_exp = sem("sp_exp")
            sp_step = sem("sp_step")
            sp_rest = sem("sp_rest")
            sp_ln = sem("sp_ln")
            sp_sum = sem("sp_sum")
            delta_ready = sem("delta_ready")
            z_mm = sem("z_mm")
            tanh_z = sem("tanh_z")
            zs_ready = sem("zs_ready")
            du_ready = sem("du_ready")
            da_ready = sem("da_ready")
            dbu_ready = sem("dbu_ready")
            h_ready = sem("h_ready")
            hc_ready = sem("hc_ready")
            n_summed = sem("n_summed")
            y_skip = sem("y_skip")
            gated = sem("gated")
            out_mm = sem("out_mm")
            res_loaded = [sem(f"res_loaded{i}") for i in range(2)]
            x2_ready = sem("x2_ready")
            x2_stat = sem("x2_stat")
            x2_stored = [sem(f"x2_stored{i}") for i in range(2)]

            def settle(engine, fence):
                engine.sem_inc(fence, 1)

            def chunk_loop(body):
                def on(engine):
                    body(engine, -1, False, True, False)
                    body(engine, 0, True, True, False)
                    with engine.Fori(1, CHUNKS - 1) as c:
                        body(engine, c, True, True, True)
                    body(engine, CHUNKS - 1, True, False, True)
                    body(engine, CHUNKS, False, False, True)
                return on

            with ExitStack() as main:
                block = main.enter_context(nc.Block())

                def sync_chunk(sp, c, scan, front, project):
                    f = c + 1
                    if front:
                        wait(sp, z_mm, JT * c)
                        settle(sp, sp_fence)
                        sp.dma_start(xn[:, f % 2, :, :], x_v[f // CB, f % CB]).then_inc(x_loaded, 16)
                    if project:
                        o = c - 1
                        for ct in range(CT + 2):
                            if ct < CT:
                                sp.wait_ge(x2_stored[ct % 2], 16 * (2 * o + ct // 2 + 1))
                                settle(sp, sp_fence)
                                sp.dma_start(xres[:, ct % 2, :],
                                             x_tile_v[o // CB, o % CB, ct]).then_inc(res_loaded[ct % 2], 16)
                            if ct >= 1 and ct - 1 < CT:
                                k = ct - 1
                                sp.wait_ge(x2_stat, CT * o + k + 1)
                                settle(sp, sp_fence)
                                sp.dma_start(x2_v[o // CB, o % CB, k],
                                             xres[:, k % 2, :]).then_inc(x2_stored[k % 2], 16)
                    if front:
                        wait(sp, dbu_ready, STEPS * c + STATE + 1)
                        settle(sp, sp_fence)
                        sp.wait_ge(dbl_ready, f + 1)
                        sp.dma_start(bc_d, dbl[RANK:64, :]).then_inc(bc_stored, 16)
                        sp.wait_ge(bc_stored, 16 * (f + 1))
                        settle(sp, sp_fence)
                        for n in range(STATE):
                            wait(sp, dbu_ready, STEPS * c + (JT - 1) * STATE + n + 1)
                            wait(sp, hc_ready, STEPS * c + (JT - 1) * STATE + n + 1)
                            for k in range(2):
                                row = STATE * k + n
                                sp.dma_start(bc[:, k, n, :],
                                             bc_d[row:row + 1, :].partition_broadcast(P)).then_inc(bc_loaded[n], 16)

                def scalar_chunk(act, c, scan, front, project):
                    f = c + 1
                    for j in range(JT):
                        for n in range(STATE):
                            tile = JT * c + j
                            step = STATE * tile + n
                            if front and j == 0 and 1 <= n <= 4:
                                ct = n - 1
                                if ct == 0:
                                    act.wait_ge(x_loaded, 16 * (f + 1))
                                    settle(act, act_fence)
                                k = (f // CB) * CT + ct
                                act.activation(xn[:, f % 2, ct, :], xn[:, f % 2, ct, :], ACT.Identity,
                                               scale=gn_scale[:, bass.ds(k, 1)],
                                               bias=gn_bias[:, bass.ds(k, 1)]).then_inc(gn_applied, 1)
                            if front and j == 0 and n in (8, 11):
                                if n == 8:
                                    act.wait_ge(centered, f + 1)
                                for ct in ((0, 1) if n == 8 else (2, 3)):
                                    wait(act, var_mm, CT * f + ct - 1)
                                    wait(act, scaled, f)
                                    settle(act, act_fence)
                                    act.activation(sq[:, ct % 2, :], xn[:, f % 2, ct, :],
                                                   ACT.Square).then_inc(squared, 1)
                            if front and j == 1 and n == 0:
                                act.wait_ge(var_mm, CT * (f + 1))
                                act.activation(sq[:, 0, :], pa[:, :], ACT.Ln, bias=eps[:, 0:1]).then_inc(rstd_guess, 1)
                                act.wait_ge(rstd_guess, 2 * f + 1)
                                act.activation(sq[:, 0, :], sq[:, 0, :], ACT.Exp,
                                               scale=-0.5).then_inc(rstd_guess, 1)
                            if front and j == 1 and 3 <= n <= 6:
                                ct = n - 3
                                if ct == 0:
                                    act.wait_ge(scaled, f + 1)
                                    settle(act, act_fence)
                                act.activation(xn[:, f % 2, ct, :], xn[:, f % 2, ct, :], ACT.Identity,
                                               scale=w_ln[:, ct:ct + 1],
                                               bias=b_ln[:, ct:ct + 1]).then_inc(xn_ready, 1)
                            if front and 3 <= j <= 6:
                                t = 2 * (j - 3) + n // 8
                                if n % 8 == 4:
                                    act.wait_ge(in_mm, JT * f + t + 1)
                                    wait(act, xs_ready, JT * f + t)
                                    act.activation(acc[:, :], pa[:, :], ACT.Identity,
                                                   scale=w_conv[:, t, TAPS - 1:TAPS],
                                                   bias=b_conv[:, t:t + 1]).then_inc(tap3, 1)
                                if n % 8 == 6:
                                    act.wait_ge(conv_step, 6 * (JT * f + t + 1))
                                    act.activation(halo[:, t, :], pa[:, T - 3:T], ACT.Copy,
                                                   scale=keep_now[:, 1:2]).then_inc(halo_saved, 1)
                                    wait(act, out_mm, CT * c)
                                    settle(act, act_fence)
                                    act.activation(xs[:, f % 2, t, :], acc[:, :], ACT.Tanh).then_inc(tanh_x, 1)
                            if front and j == 7 and n == 4:
                                act.wait_ge(x_mm, f + 1)
                                wait(act, dt_mm, JT * f)
                                wait(act, bc_stored, 16 * f)
                                act.activation(dbl[:, :], pa[0:64, :], ACT.Copy).then_inc(dbl_ready, 1)
                            first = 8 if j == 7 else 1
                            if front if j == 7 else scan:
                                nt = tile + 1
                                dt_ps = pout if j == 7 else pb
                                jn = (j + 1) % JT
                                if n == first:
                                    act.wait_ge(dt_mm, nt + 1)
                                    wait(act, delta_ready, nt)
                                    act.activation(sp_e[:, :], dt_ps[:, :], ACT.Abs,
                                                   bias=b_dt[:, jn:jn + 1]).then_inc(sp_exp, 1)
                                    act.activation(sp_m[:, :], dt_ps[:, :], ACT.Relu,
                                                   bias=b_dt[:, jn:jn + 1]).then_inc(dt_read, 1)
                                if n == first + 1:
                                    act.wait_ge(sp_exp, 2 * nt + 1)
                                    act.activation(sp_e[:, :], sp_e[:, :], ACT.Exp, scale=-1.0).then_inc(sp_exp, 1)
                                    act.wait_ge(sp_exp, 2 * nt + 2)
                                    act.activation(sp_w[:, :], sp_e[:, :], ACT.Identity,
                                                   bias=one[:, 0:1]).then_inc(sp_step, 1)
                                if n == first + 3:
                                    act.wait_ge(sp_rest, nt + 1)
                                    act.activation(sp_e[:, :], sp_e[:, :], ACT.Ln, bias=one[:, 0:1]).then_inc(sp_ln, 1)
                            if scan and n == 8:
                                act.wait_ge(z_mm, tile + 1)
                                wait(act, gated, tile)
                                act.activation(zs[:, :], pb[:, :], ACT.Tanh).then_inc(tanh_z, 1)
                            if scan and n > 0 or (j > 0 and scan):
                                prev = step - 1
                                col = STATE * j + n - 1
                                act.wait_ge(h_ready, prev + 1)
                                act.activation(carry[:, col:col + 1], hs[:, (n - 1) % H_RING, T - 1:T], ACT.Copy,
                                               scale=keep_now[:, 0:1]).then_inc(carried, 1)
                            if scan and j == 0 and n == 0 and not (isinstance(c, int) and c == 0):
                                act.wait_ge(h_ready, step)
                                act.activation(carry[:, STEPS - 1:STEPS], hs[:, H_RING - 1, T - 1:T], ACT.Copy,
                                               scale=keep_now[:, 0:1]).then_inc(carried, 1)
                            if (scan or front) and j == 0 and n == 0:
                                wait(act, carried, STEPS * c)
                                wait(act, halo_saved, JT * f)
                                act.activation(keep_now[:, :], keep[:, bass.ds(c + 1, 2)], ACT.Copy).then_inc(keep_set, 1)
                                act.wait_ge(keep_set, c + 2)
                            last = j == JT - 1 and n == STATE - 1
                            if (scan and not last) or (last and front):
                                nn, jn = (n + 1) % STATE, (j + (n + 1) // STATE) % JT
                                if nn == 0:
                                    act.wait_ge(delta_ready, tile + 2)
                                wait(act, h_ready, step)
                                act.activation(da_ps[nn % DA_RING][:, :], delta[:, jn % 2, :], ACT.Exp,
                                               scale=neg_a[:, jn, nn:nn + 1]).then_inc(da_ready, 1)

                def vector_chunk(dve, c, scan, front, project):
                    f = c + 1
                    for j in range(JT):
                        for n in range(STATE):
                            tile = JT * c + j
                            step = STATE * tile + n
                            if front and j == 0 and n == 7:
                                dve.wait_ge(mean_mm, f + 1)
                                dve.tensor_tensor(xn[:, f % 2, :, :], xn[:, f % 2, :, :],
                                                  pa[:, :].unsqueeze(1).broadcast_to([P, CT, T]),
                                                  ALU.subtract).then_inc(centered, 1)
                            if front and j == 1 and n == 1:
                                dve.wait_ge(rstd_guess, 2 * f + 2)
                                dve.tensor_tensor(sq[:, 1, :], sq[:, 0, :], sq[:, 0, :], ALU.mult).then_inc(newton, 1)
                                dve.wait_ge(newton, 4 * f + 1)
                                dve.scalar_tensor_tensor(sq[:, 1, :], pa[:, :], LN_EPS, sq[:, 1, :], ALU.add,
                                                         ALU.mult).then_inc(newton, 1)
                                dve.wait_ge(newton, 4 * f + 2)
                                dve.tensor_scalar(sq[:, 1, :], sq[:, 1, :], -0.5, 1.5, ALU.mult,
                                                  ALU.add).then_inc(newton, 1)
                                dve.wait_ge(newton, 4 * f + 3)
                                dve.tensor_tensor(sq[:, 0, :], sq[:, 0, :], sq[:, 1, :], ALU.mult).then_inc(newton, 1)
                            if front and j == 1 and n == 2:
                                dve.wait_ge(newton, 4 * f + 4)
                                dve.tensor_tensor(xn[:, f % 2, :, :], xn[:, f % 2, :, :],
                                                  sq[:, 0:1, :].broadcast_to([P, CT, T]),
                                                  ALU.mult).then_inc(scaled, 1)
                            if front and 3 <= j <= 6:
                                t = 2 * (j - 3) + n // 8
                                if n % 8 == 5:
                                    dve.wait_ge(tap3, JT * f + t + 1)
                                    wait(dve, halo_saved, JT * (f - 1) + t + 1)
                                    k = 6 * (JT * f + t)
                                    for s in range(1, TAPS):
                                        wait(dve, conv_step, k + 2 * (s - 1))
                                        w = w_conv[:, t, TAPS - 1 - s:TAPS - s]
                                        dve.scalar_tensor_tensor(acc[:, s:T], pa[:, 0:T - s], w, acc[:, s:T], ALU.mult,
                                                                 ALU.add).then_inc(conv_step, 1)
                                        dve.scalar_tensor_tensor(acc[:, 0:s], halo[:, t, TAPS - 1 - s:TAPS - 1], w,
                                                                 acc[:, 0:s], ALU.mult,
                                                                 ALU.add).then_inc(conv_step, 1)
                                if n % 8 == 7:
                                    dve.wait_ge(tanh_x, JT * f + t + 1)
                                    half = xs[:, f % 2, t, :]
                                    dve.scalar_tensor_tensor(half, half, 1.0, acc[:, :], ALU.add,
                                                             ALU.mult).then_inc(xs_ready, 1)
                            first = 8 if j == 7 else 1
                            if (front if j == 7 else scan) and n == first + 2:
                                dve.wait_ge(sp_step, tile + 2)
                                dve.scalar_tensor_tensor(sp_w[:, :], sp_w[:, :], 1.0, sp_e[:, :], ALU.subtract,
                                                         ALU.subtract).then_inc(sp_rest, 1)
                            if scan and n == 9:
                                dve.wait_ge(tanh_z, tile + 1)
                                dve.scalar_tensor_tensor(zs[:, :], zs[:, :], 1.0, pb[:, :], ALU.add,
                                                         ALU.mult).then_inc(zs_ready, 1)
                            if n == 3 and ((scan and j > 0) or (project and j == 0)):
                                jp, o = (j - 1) % JT, (c if j > 0 else c - 1)
                                dve.wait_ge(n_summed, STATE * tile)
                                dve.scalar_tensor_tensor(xs[:, o % 2, jp, :], xs[:, o % 2, jp, :], skip[:, jp:jp + 1],
                                                         y_ps[jp % 2][:, :], ALU.mult, ALU.add).then_inc(y_skip, 1)
                            if project and (j, n) in ((1, 1), (1, 11), (2, 5), (2, 15)):
                                ct = ((1, 1), (1, 11), (2, 5), (2, 15)).index((j, n))
                                o = c - 1
                                dve.wait_ge(out_mm, CT * o + ct + 1)
                                dve.wait_ge(res_loaded[ct % 2], 16 * (2 * o + ct // 2 + 1))
                                dve.tensor_tensor(xres[:, ct % 2, :], pout[:, :], xres[:, ct % 2, :],
                                                  ALU.add).then_inc(x2_ready, 1)
                                dve.wait_ge(x2_ready, CT * o + ct + 1)
                                dve.bn_stats(x2_stats[:, ct, bass.ds(o, 1), :].rearrange("p a s -> p (a s)"),
                                             xres[:, ct % 2, :]).then_inc(x2_stat, 1)
                            last = j == JT - 1 and n == STATE - 1
                            if (scan and not last) or (last and front):
                                nn, jn = (n + 1) % STATE, (j + (n + 1) // STATE) % JT
                                cn = c + 1 if last else c
                                if nn == 0:
                                    wait(dve, dbu_ready, step + 1)
                                    dve.wait_ge(delta_ready, tile + 2)
                                    wait(dve, xs_ready, JT * cn + jn + 1)
                                    dve.tensor_tensor(du_ps[:, :], delta[:, jn % 2, :], xs[:, cn % 2, jn, :],
                                                      ALU.mult).then_inc(du_ready, 1)
                                    dve.wait_ge(du_ready, tile + 2)
                                if jn == 0:
                                    dve.wait_ge(bc_loaded[nn], 32 * (cn + 1))
                                wait(dve, hc_ready, step + 2 - H_RING)
                                dve.tensor_tensor(hs[:, nn % H_RING, :], du_ps[:, :], bc[:, 0, nn, :],
                                                  ALU.mult).then_inc(dbu_ready, 1)
                            if scan:
                                dve.wait_ge(da_ready, step + 1)
                                dve.wait_ge(dbu_ready, step + 1)
                                dve.tensor_tensor_scan(hs[:, n % H_RING, :], da_ps[n % DA_RING][:, :],
                                                       hs[:, n % H_RING, :],
                                                       carry[:, STATE * j + n:STATE * j + n + 1], ALU.mult,
                                                       ALU.add).then_inc(h_ready, 1)

                def gpsimd_chunk(pool, c, scan, front, project):
                    for j in range(JT):
                        for n in range(STATE):
                            tile = JT * c + j
                            step = STATE * tile + n
                            first = 8 if j == 7 else 1
                            if (front if j == 7 else scan) and n == first + 4:
                                nt = tile + 1
                                pool.wait_ge(sp_ln, nt + 1)
                                pool.tensor_tensor(sp_m[:, :], sp_m[:, :], sp_e[:, :], ALU.add).then_inc(sp_sum, 1)
                                pool.wait_ge(sp_sum, nt + 1)
                                wait(pool, da_ready, STATE * (nt - 1))
                                wait(pool, du_ready, nt - 1)
                                pool.tensor_tensor(delta[:, (j + 1) % 2, :], sp_m[:, :], sp_w[:, :],
                                                   ALU.subtract).then_inc(delta_ready, 1)
                            if n == 4 and ((scan and j > 0) or (project and j == 0)):
                                jp, o = (j - 1) % JT, (c if j > 0 else c - 1)
                                pool.wait_ge(y_skip, tile)
                                pool.wait_ge(zs_ready, tile)
                                pool.tensor_tensor(xs[:, o % 2, jp, :], xs[:, o % 2, jp, :], zs[:, :],
                                                   ALU.mult).then_inc(gated, 1)
                            if scan:
                                pool.wait_ge(h_ready, step + 1)
                                wait(pool, n_summed, step + 1 - HC_RING)
                                pool.tensor_tensor(hc[:, n % HC_RING, :], hs[:, n % H_RING, :], bc[:, 1, n, :],
                                                   ALU.mult).then_inc(hc_ready, 1)

                def tensor_chunk(pe, c, scan, front, project):
                    f = c + 1
                    for j in range(JT):
                        for n in range(STATE):
                            tile = JT * c + j
                            step = STATE * tile + n
                            if front and j == 0 and 3 <= n <= 6:
                                ct = n - 3
                                pe.wait_ge(gn_applied, CT * f + ct + 1)
                                if ct == 0:
                                    wait(pe, dbl_ready, f)
                                mm = pe.matmul(pa[:, :], channel_mean[:, :], xn[:, f % 2, ct, :], start=ct == 0,
                                               stop=ct == CT - 1)
                                if ct == CT - 1:
                                    mm.then_inc(mean_mm, 1)
                            if front and j == 0 and n in (9, 10, 12, 13):
                                ct = (9, 10, 12, 13).index(n)
                                pe.wait_ge(squared, CT * f + ct + 1)
                                pe.matmul(pa[:, :], channel_mean[:, :], sq[:, ct % 2, :], start=ct == 0,
                                          stop=ct == CT - 1).then_inc(var_mm, 1)
                            if front and 3 <= j <= 6 and n % 8 < CT:
                                t, ct = 2 * (j - 3) + n // 8, n % 8
                                if ct == 0 and t == 0:
                                    pe.wait_ge(xn_ready, CT * (f + 1))
                                    pe.wait_ge(newton, 4 * f + 2)
                                elif ct == 0:
                                    pe.wait_ge(halo_saved, JT * f + t)
                                mm = pe.matmul(pa[:, :], w_in[:, ct, t * P:(t + 1) * P], xn[:, f % 2, ct, :],
                                               start=ct == 0, stop=ct == CT - 1)
                                if ct == CT - 1:
                                    mm.then_inc(in_mm, 1)
                            if front and j == 7 and n < 4:
                                if n == 0:
                                    pe.wait_ge(halo_saved, JT * (f + 1))
                                for t in (2 * n, 2 * n + 1):
                                    pe.wait_ge(xs_ready, JT * f + t + 1)
                                    mm = pe.matmul(pa[0:64, :], w_x[:, t, :], xs[:, f % 2, t, :], start=t == 0,
                                                   stop=t == JT - 1)
                                if n == 3:
                                    mm.then_inc(x_mm, 1)
                            if scan and j < 7 and n == 0:
                                wait(pe, zs_ready, tile)
                                pe.matmul(pb[:, :], w_dt[:, (j + 1) * P:(j + 2) * P], dbl[0:RANK, :], start=True,
                                          stop=True).then_inc(dt_mm, 1)
                            if front and j == 7 and n == 6:
                                pe.wait_ge(dbl_ready, f + 1)
                                wait(pe, x2_ready, CT * c)
                                pe.matmul(pout[:, :], w_dt[:, 0:P], dbl[0:RANK, :], start=True,
                                          stop=True).then_inc(dt_mm, 1)
                            if scan and 4 <= n < 4 + CT:
                                ct = n - 4
                                if ct == 0:
                                    pe.wait_ge(dt_read, tile + 1 + (j < 7))
                                    wait(pe, zs_ready, tile)
                                lo = INNER + j * P
                                mm = pe.matmul(pb[:, :], w_in[:, ct, lo:lo + P], xn[:, c % 2, ct, :], start=ct == 0,
                                               stop=ct == CT - 1)
                                if ct == CT - 1:
                                    mm.then_inc(z_mm, 1)
                            slot = STATE * j + n
                            if project and 8 <= slot < 8 + 10 * CT and (slot - 8) % 10 < JT:
                                ct, k = divmod(slot - 8, 10)
                                o = c - 1
                                if k == 0 and ct == 0:
                                    pe.wait_ge(gated, JT * c)
                                    if scan:
                                        pe.wait_ge(dt_read, JT * c + 1)
                                elif k == 0:
                                    pe.wait_ge(x2_ready, CT * o + ct)
                                mm = pe.matmul(pout[:, :], w_out[:, k, ct * P:(ct + 1) * P], xs[:, o % 2, k, :],
                                               start=k == 0, stop=k == JT - 1)
                                if k == JT - 1:
                                    mm.then_inc(out_mm, 1)
                            if scan:
                                pe.wait_ge(hc_ready, step + 1)
                                if n == 0:
                                    wait(pe, y_skip, tile - 1)
                                pe.matmul(y_ps[j % 2][:, :], identity[:, :], hc[:, n % HC_RING, :], start=n == 0,
                                          stop=n == STATE - 1).then_inc(n_summed, 1)

                @block.sync
                def _(sp):
                    for i in range(2):
                        sp.sem_inc(x2_stored[i], 16)
                    chunk_loop(sync_chunk)(sp)
                    for i in range(2):
                        sp.wait_ge(x2_stored[i], 16 * (CHUNKS * CT // 2 + 1))

                @block.scalar
                def _(act):
                    chunk_loop(scalar_chunk)(act)

                @block.vector
                def _(dve):
                    chunk_loop(vector_chunk)(dve)

                @block.gpsimd
                def _(pool):
                    chunk_loop(gpsimd_chunk)(pool)

                @block.tensor
                def _(pe):
                    chunk_loop(tensor_chunk)(pe)

        layer1 = ExitStack()
        with layer1:
            w_k = sb("w_k", [P, CT, DIM], layer1)
            w_v = sb("w_v", [P, CT, DIM], layer1)
            w_q = sb("w_q", [P, CT, DIM], layer1)
            w_o = sb("w_o", [P, CT, DIM], layer1)
            b_o = sb("b_o", [P, CT], layer1)
            gn1_scale = sb("gn1_scale", [P, BATCH * CT], layer1)
            gn1_bias = sb("gn1_bias", [P, BATCH * CT], layer1)
            keys = sb("keys", [P, CT, TOKENS], layer1)
            xl = sb("xl", [P, 2, CT, T], layer1)
            xg = sb("xg", [P, 2, CT, T], layer1)
            ek = sb("ek", [P, 2, CT, T], layer1)
            v_t = sb("v_t", [P, 2, DIM], layer1)
            ek_t = sb("ek_t", [P, 2, DIM], layer1)
            key_max = sb("key_max", [P, CT, CB], layer1)
            neg_max = sb("neg_max", [P, CT], layer1)
            key_sum = sb("key_sum", [P, CT, CB], layer1)
            inv_sum = sb("inv_sum", [P, CT], layer1)
            context = sb("context", [P, CT, P], layer1)
            g_sb = sb("g_sb", [P, CT, DIM], layer1)
            m_sb = sb("m_sb", [P, CT, DIM], layer1)
            banks = [layer1.enter_context(nc.psum_tensor(f"l1_bank{i}", [P, T], FP32)) for i in range(8)]

            w1_loaded, w1_rest_loaded = sem("w1_loaded"), sem("w1_rest_loaded")
            gn1_done, zeroed = sem("gn1_done"), sem("zeroed")
            loaded = [sem(f"loaded{u}") for u in range(2)]
            stored = [sem(f"stored{u}") for u in range(2)]
            normed = sem("normed")
            xg_used = sem("xg_used")
            k_mm, k_copied, k_maxed = sem("k_mm"), sem("k_copied"), sem("k_maxed")
            max_step, max_ready = sem("max_step"), sem("max_ready")
            exp_done = sem("exp_done")
            v_mm, v_copied = sem("v_mm"), sem("v_copied")
            tr_mm, ek_copied = sem("tr_mm"), sem("ek_copied")
            ctx_mm, ctx_copied = sem("ctx_mm"), sem("ctx_copied")
            sum_step = sem("sum_step")
            g_mm, g_ready = sem("g_mm"), sem("g_ready")
            m_mm, m_ready = sem("m_mm"), sem("m_ready")
            y_mm, y_ready = sem("y_mm"), sem("y_ready")
            sp1_fence, dve_fence = sem("sp1_fence"), sem("dve_fence")

            PAIRS = CB // 2
            KEYS, VALUES, OUTPUT = range(3)
            out_v = out.rearrange("b (ct p) (cb t) -> b cb p ct t", p=P, t=T)

            def pass_loop(pair, b, number):
                def on(engine):
                    pair(engine, b, number, 0)
                    with engine.Fori(1, PAIRS - 1) as i:
                        pair(engine, b, number, i)
                    pair(engine, b, number, PAIRS - 1)
                return on

            with ExitStack() as stack:
                block = stack.enter_context(nc.Block())
                gc_vector, gc_tensor, gc_scalar = group_coefficients(
                    nc, stack, block, "gn1",
                    lambda i: x2_stats[:, i % CT, (i // CT) * CB:(i // CT + 1) * CB, :].rearrange("p c s -> p (c s)"),
                    BATCH * CT, CB, averages[:, :], banks[0], gn1_scale[:, :], gn1_bias[:, :])

                @block.sync
                def _(sp):
                    def load(b, cb, u, count):
                        sp.dma_start(xl[:, u, :, :], x2_d[b].rearrange("(ct p) (cb t) -> cb p ct t", p=P, t=T)[cb]
                                     ).then_inc(loaded[u], 16)

                    sp.dma_start(w_k[:, :, :], qkv[:, DIM:2 * DIM].rearrange("(ct p) n -> p ct n", p=P)
                                 ).then_inc(w1_loaded, 16)
                    load(0, 0, 0, 0)
                    sp.dma_start(w_v[:, :, :], qkv[:, 2 * DIM:].rearrange("(ct p) n -> p ct n", p=P)
                                 ).then_inc(w1_rest_loaded, 16)
                    sp.dma_start(w_q[:, :, :], q_rows.rearrange("(m p) n -> p m n", p=P)).then_inc(w1_rest_loaded, 16)
                    sp.dma_start(w_o[:, :, :], w_out1.rearrange("(m p) n -> p m n", p=P)).then_inc(w1_rest_loaded, 16)
                    sp.dma_start(b_o[:, :], b_out1).then_inc(w1_rest_loaded, 16)

                    def pair(sp, b, number, i):
                        for u in range(2):
                            a, q = CB * b + 2 * i + u, 3 * CB * b + CB * number + 2 * i + u
                            same = not (isinstance(i, int) and i == PAIRS - 1 and u == 1)
                            nb, ncb = (b, 2 * i + u + 1) if same else (b + (number == OUTPUT), 0)
                            if nb < BATCH:
                                wait(sp, normed, CT * q)
                                if number == OUTPUT and not (isinstance(i, int) and i == 0 and u == 0):
                                    settle(sp, sp1_fence)
                                    sp.wait_ge(stored[1 - u], 16 * ((a - 1) // 2 + 1) if isinstance(a, int) else
                                               16 * (PAIRS * b + i + u))
                                settle(sp, sp1_fence)
                                load(nb, ncb, 1 - u, None)
                            if number == OUTPUT:
                                sp.wait_ge(y_ready, CT * (a + 1))
                                settle(sp, sp1_fence)
                                sp.dma_start(out_v[b, 2 * i + u], xl[:, u, :, :]).then_inc(stored[u], 16)

                    for b in range(BATCH):
                        for number in (KEYS, VALUES, OUTPUT):
                            pass_loop(pair, b, number)(sp)
                    for u in range(2):
                        sp.wait_ge(stored[u], 16 * BATCH * PAIRS)

                @block.gpsimd
                def _(pool):
                    pool.memset(context[:, :, :], 0.0).then_inc(zeroed, 1)

                @block.scalar
                def _(act):
                    gc_scalar(act)

                    def normalize(b, u, q):
                        wait(act, xg_used, q - 1)
                        for ct in range(CT):
                            k = CT * b + ct
                            act.activation(xg[:, u, ct, :], xl[:, u, ct, :], ACT.Identity, scale=gn1_scale[:, k:k + 1],
                                           bias=gn1_bias[:, k:k + 1]).then_inc(normed, 1)

                    act.wait_ge(gn1_done, 1)
                    act.wait_ge(loaded[0], 16)
                    normalize(0, 0, 0)

                    def pair(act, b, number, i):
                        for u in range(2):
                            a, q = CB * b + 2 * i + u, 3 * CB * b + CB * number + 2 * i + u
                            cb = 2 * i + u
                            same = not (isinstance(i, int) and i == PAIRS - 1 and u == 1)
                            nb = b if same else b + (number == OUTPUT)
                            if nb < BATCH:
                                half = 3 * PAIRS * b + PAIRS * number + i + u
                                act.wait_ge(loaded[1 - u], 16 * (half + 1))
                                normalize(nb, 1 - u, q + 1)
                            if number == KEYS:
                                for m in range(CT):
                                    act.wait_ge(k_mm, CT * a + m + 1)
                                    settle(act, act_fence)
                                    act.activation(keys[:, m, bass.ds(cb * T, T)], banks[m % 2][:, :],
                                                   ACT.Copy).then_inc(k_copied, 1)
                            if number == VALUES:
                                wait(act, tr_mm, CT * (a - 1))
                                settle(act, act_fence)
                                for m in range(CT):
                                    act.activation(ek[:, u, m, :], keys[:, m, bass.ds(cb * T, T)], ACT.Exp,
                                                   bias=neg_max[:, m:m + 1],
                                                   accum_out=key_sum[:, m, bass.ds(cb, 1)]).then_inc(exp_done, 1)
                                for lb in range(CT):
                                    block_no = CT * a + lb
                                    act.wait_ge(v_mm, block_no + 1)
                                    wait(act, ctx_mm, block_no - 1)
                                    act.activation(v_t[:, lb % 2, :], banks[lb % 2][:, :],
                                                   ACT.Copy).then_inc(v_copied, 1)

                    for b in range(BATCH):
                        pass_loop(pair, b, KEYS)(act)
                        act.wait_ge(k_copied, CT * CB * (b + 1))
                        act.wait_ge(max_ready, b + 1)
                        pass_loop(pair, b, VALUES)(act)
                        wait(act, y_mm, CT * CB * b)
                        for ct in range(CT):
                            act.wait_ge(m_mm, CT * b + ct + 1)
                            act.activation(m_sb[:, ct, :], banks[ct][:, :], ACT.Copy).then_inc(m_ready, 1)
                        pass_loop(pair, b, OUTPUT)(act)

                @block.vector
                def _(dve):
                    gc_vector(dve, gn1_done)
                    dve.wait_ge(w1_rest_loaded, 64)
                    dve.wait_ge(zeroed, 1)

                    def pair(dve, b, number, i):
                        for u in range(2):
                            a = CB * b + 2 * i + u
                            cb = 2 * i + u
                            if number == KEYS:
                                for m in range(CT):
                                    dve.wait_ge(k_copied, CT * a + m + 1)
                                    settle(dve, dve_fence)
                                    dve.tensor_reduce(key_max[:, m, bass.ds(cb, 1)],
                                                      keys[:, m, bass.ds(cb * T, T)], AX.X,
                                                      ALU.max).then_inc(k_maxed, 1)
                            if number == VALUES:
                                for lb in range(CT):
                                    block_no = CT * a + lb
                                    dve.wait_ge(tr_mm, block_no + 1)
                                    wait(dve, ctx_mm, block_no - 1)
                                    dve.tensor_copy(ek_t[:, lb % 2, :], banks[2 + lb % 2][:, :]).then_inc(ek_copied, 1)
                            if number == OUTPUT:
                                for o in range(CT):
                                    dve.wait_ge(y_mm, CT * a + o + 1)
                                    dve.scalar_tensor_tensor(xl[:, u, o, :], banks[o][:, :], b_o[:, o:o + 1],
                                                             xl[:, u, o, :], ALU.add, ALU.add).then_inc(y_ready, 1)

                    for b in range(BATCH):
                        pass_loop(pair, b, KEYS)(dve)
                        dve.wait_ge(k_maxed, CT * CB * (b + 1))
                        dve.tensor_reduce(neg_max[:, :], key_max[:, :, :], AX.X, ALU.max).then_inc(max_step, 1)
                        dve.wait_ge(max_step, b + 1)
                        dve.tensor_scalar(neg_max[:, :], neg_max[:, :], -1.0, None, ALU.mult).then_inc(max_ready, 1)
                        pass_loop(pair, b, VALUES)(dve)
                        dve.wait_ge(exp_done, CT * CB * (b + 1))
                        dve.tensor_reduce(inv_sum[:, :], key_sum[:, :, :], AX.X, ALU.add).then_inc(sum_step, 1)
                        dve.wait_ge(sum_step, 2 * b + 1)
                        dve.reciprocal(inv_sum[:, :], inv_sum[:, :]).then_inc(sum_step, 1)
                        dve.wait_ge(ctx_mm, CT * CB * (b + 1))
                        for m in range(CT):
                            for lo in (0, 64):
                                dve.tensor_copy(context[lo:lo + 64, m, lo:lo + 64],
                                                banks[4 + m][lo:lo + 64, lo:lo + 64]).then_inc(ctx_copied, 1)
                        dve.wait_ge(sum_step, 2 * b + 2)
                        wait(dve, m_mm, CT * b)
                        for m in range(CT):
                            dve.wait_ge(g_mm, CT * b + m + 1)
                            dve.tensor_scalar(g_sb[:, m, :], banks[m][:, :], inv_sum[:, m:m + 1], None,
                                              ALU.mult).then_inc(g_ready, 1)
                        pass_loop(pair, b, OUTPUT)(dve)

                @block.tensor
                def _(pe):
                    gc_tensor(pe)
                    pe.wait_ge(w1_loaded, 16)
                    pe.wait_ge(gn1_done, 1)

                    def context_products(block_no, lb, start, stop):
                        pe.wait_ge(v_copied, block_no + 1)
                        pe.wait_ge(ek_copied, block_no + 1)
                        for m in range(CT):
                            mm = pe.matmul(banks[4 + m][:, 0:P], v_t[:, lb % 2, m * P:(m + 1) * P],
                                           ek_t[:, lb % 2, m * P:(m + 1) * P], start=start, stop=stop)
                        mm.then_inc(ctx_mm, 1)

                    def pair(pe, b, number, i):
                        for u in range(2):
                            a, q = CB * b + 2 * i + u, 3 * CB * b + CB * number + 2 * i + u
                            pe.wait_ge(normed, CT * (q + 1))
                            if number == KEYS:
                                for m in range(CT):
                                    wait(pe, k_copied, CT * a + m - 1)
                                    for ct in range(CT):
                                        mm = pe.matmul(banks[m % 2][:, :], w_k[:, ct, m * P:(m + 1) * P],
                                                       xg[:, u, ct, :], start=ct == 0, stop=ct == CT - 1)
                                    mm.then_inc(k_mm, 1)
                                pe.wait_ge(k_mm, CT * (a + 1))
                                pe.sem_inc(xg_used, 1)
                            if number == VALUES:
                                for lb in range(CT):
                                    block_no = CT * a + lb
                                    wait(pe, v_copied, block_no - 1)
                                    for ct in range(CT):
                                        mm = pe.matmul(banks[lb % 2][:, :], xg[:, u, ct, lb * P:(lb + 1) * P],
                                                       w_v[:, ct, :], start=ct == 0, stop=ct == CT - 1)
                                    mm.then_inc(v_mm, 1)
                                    if lb == 0:
                                        pe.wait_ge(exp_done, CT * (a + 1))
                                    wait(pe, ek_copied, block_no - 1)
                                    for m in range(CT):
                                        mm = pe.transpose(banks[2 + lb % 2][:, m * P:(m + 1) * P],
                                                          ek[:, u, m, lb * P:(lb + 1) * P], identity[:, :])
                                    mm.then_inc(tr_mm, 1)
                                    first = isinstance(i, int) and i == 0 and u == 0
                                    if not (first and lb == 0):
                                        context_products(block_no - 1, lb - 1, first and lb == 1, False)
                                pe.wait_ge(tr_mm, CT * (a + 1))
                                pe.sem_inc(xg_used, 1)
                            if number == OUTPUT:
                                for o in range(CT):
                                    wait(pe, y_ready, CT * (a - 1) + o + 1)
                                    for ct in range(CT):
                                        mm = pe.matmul(banks[o][:, :], m_sb[:, ct, o * P:(o + 1) * P],
                                                       xg[:, u, ct, :], start=ct == 0, stop=ct == CT - 1)
                                    mm.then_inc(y_mm, 1)
                                pe.wait_ge(y_mm, CT * (a + 1))
                                pe.sem_inc(xg_used, 1)

                    for b in range(BATCH):
                        wait(pe, y_ready, CT * CB * b)
                        pass_loop(pair, b, KEYS)(pe)
                        pe.wait_ge(k_copied, CT * CB * (b + 1))
                        pe.wait_ge(w1_rest_loaded, 64)
                        wait(pe, ctx_copied, 2 * CT * b)
                        pass_loop(pair, b, VALUES)(pe)
                        context_products(CT * CB * (b + 1) - 1, CT - 1, False, True)
                        for m in range(CT):
                            pe.wait_ge(ctx_copied, 2 * CT * b + 2 * m + 2)
                            pe.matmul(banks[m][:, :], context[:, m, :], w_o[:, m, :], start=True,
                                      stop=True).then_inc(g_mm, 1)
                        pe.wait_ge(g_ready, CT * (b + 1))
                        for ct in range(CT):
                            for m in range(CT):
                                mm = pe.matmul(banks[ct][:, :], w_q[:, m, ct * P:(ct + 1) * P], g_sb[:, m, :],
                                               start=m == 0, stop=m == CT - 1)
                            mm.then_inc(m_mm, 1)
                        pe.wait_ge(m_ready, CT * (b + 1))
                        pass_loop(pair, b, OUTPUT)(pe)


def kernel(**inputs):
    import numpy as _np
    import concourse.bacc as _bacc
    from concourse import mybir as _mybir
    from concourse.bass_utils import run_bass_kernel_spmd as _run

    def rows(v, k):
        v = _np.asarray(v)
        return _np.ascontiguousarray(_np.moveaxis(v.reshape((k, 128) + v.shape[1:]), 0, 1))

    g = {k: _np.asarray(v) for k, v in inputs.items()}
    laid = {
        "x": g["x"].reshape(2, 512, 4096),
        "ln_w": rows(g["L0_conv_ln_w"], 4),
        "ln_b": rows(g["L0_conv_ln_b"], 4),
        "in_proj": g["L0_conv_in_proj_w"].T,
        "conv_w": rows(g["L0_conv_conv_w"], 8),
        "conv_b": rows(g["L0_conv_conv_b"], 8),
        "x_proj": g["L0_conv_x_proj_w"].T,
        "dt_proj": g["L0_conv_dt_proj_w"].T,
        "dt_b": rows(g["L0_conv_dt_proj_b"], 8),
        "a_log": rows(g["L0_conv_A_log"], 8),
        "d_skip": rows(g["L0_conv_D_skip"], 8),
        "out_proj": g["L0_conv_out_proj_w"].T,
        "qkv": g["L1_conv_w_qkv"].T,
        "q_rows": g["L1_conv_w_qkv"][:512],
        "w_out1": g["L1_conv_w_out"].T,
        "b_out1": rows(g["L1_conv_b_out"], 4),
    }
    nc = _bacc.Bacc("TRN2", target_bir_lowering=False, num_devices=1)
    arrays, args = {}, []
    for name, a in laid.items():
        a = _np.ascontiguousarray(a)
        arrays[f"in_{name}"] = a
        args.append(nc.dram_tensor(f"in_{name}", a.shape, _mybir.dt.from_np(a.dtype), kind="ExternalInput").ap())
    args.append(nc.dram_tensor("out_0", (2, 512, 4096), _mybir.dt.float32, kind="ExternalOutput").ap())
    mamba_and_linear_attention(nc, *args)
    r = _run(nc, [arrays], core_ids=[0])
    return r.results[0]["out_0"].reshape(2, 512, 64, 64)
```

```python
import concourse.bass as bass
from concourse import mybir
from concourse.alu_op_type import AluOpType
from contextlib import ExitStack

FP32 = mybir.dt.float32
FP32R = mybir.dt.float32r
ALU = mybir.AluOpType
ACT = mybir.ActivationFunctionType
AX = mybir.AxisListType

P = 128
BATCH, DIM, TOKENS = 2, 512, 4096
CT = DIM // P
T = 512
CB = TOKENS // T
CHUNKS = BATCH * CB
INNER, STATE, TAPS, RANK = 1024, 16, 4, 32
JT = INNER // P
STEPS = JT * STATE
GROUP = DIM // 32
LN_EPS = 1e-5
GN_EPS = 1e-5
H_RING, HC_RING, DA_RING = 8, 4, 3
SUM_LAG = 2

NORM, MEAN, CENTER = (4, 5, 9, 10), (6, 7, 10, 11), 15
SQUARE, VARIANCE = (17, 20), (17, 18, 20, 21)
RSTD, NEWTON, SCALE, AFFINE = 24, 26, 27, 29
OUT_MM = (tuple(range(6, 14)), (17, *range(20, 27)), tuple(range(27, 35)), (33, *range(36, 43)))
OUT_ADD = (17, 30, 39, 47)
IN_MM = tuple(42 + 8 * t for t in range(JT))
TAP3, CONV, TANH, SILU = 6, 8, 10, 12
X_MM, DBL, DT_SPLIT = (107, 108, 109, 111), 113, 114
DT_MM, SP_ABS, SP_EXP, SP_ROUND, SP_LN, SP_REST, SP_SUM, SP_DELTA = 14, 1, 3, 4, 6, 7, 9, 10
DT_MM7, SP_ABS7, SP_EXP7, SP_ROUND7, SP_LN7, SP_REST7, SP_SUM7, SP_DELTA7 = 3, 6, 7, 8, 9, 10, 11, 12
Z_MM, Z_TANH, Z_SILU = (2, 2, 2, 3), 8, 11
Y_SKIP, Y_GATE = 3, 5


def wait(engine, sem, value):
    if isinstance(value, int) and value <= 0:
        return
    engine.wait_ge(sem, value)


def group_coefficients(nc, ctx, block, name, stats, tiles, per_tile, averages, psum, scale, bias):
    mv = ctx.enter_context(nc.sbuf_tensor(f"{name}_mean_var", [P, tiles, 2], FP32))
    gm = ctx.enter_context(nc.sbuf_tensor(f"{name}_group_mean", [P, tiles], FP32))
    dev = ctx.enter_context(nc.sbuf_tensor(f"{name}_spread", [P, tiles], FP32))
    gv = ctx.enter_context(nc.sbuf_tensor(f"{name}_group_var", [P, tiles], FP32))
    tmp = ctx.enter_context(nc.sbuf_tensor(f"{name}_tmp", [P, tiles], FP32))
    v_step = ctx.enter_context(nc.semaphore(f"{name}_v_step"))
    mean_mm = ctx.enter_context(nc.semaphore(f"{name}_mean_mm"))
    var_mm = ctx.enter_context(nc.semaphore(f"{name}_var_mm"))
    a_step = ctx.enter_context(nc.semaphore(f"{name}_a_step"))
    mean_ps, var_ps = psum[:, 0:tiles], psum[:, 64:64 + tiles]

    def vector(dve, done):
        count = [0]

        def step(instruction):
            count[0] += 1
            instruction.then_inc(v_step, 1)
            dve.wait_ge(v_step, count[0])

        for i in range(tiles):
            last = dve.bn_aggr(mv[:, i, :], stats(i))
            if i < tiles - 1:
                last.then_inc(v_step, 1)
                count[0] += 1
        step(last)
        dve.wait_ge(mean_mm, 1)
        step(dve.tensor_copy(gm[:, :], mean_ps))
        step(dve.tensor_tensor(dev[:, :], mv[:, :, 0], gm[:, :], ALU.subtract))
        step(dve.tensor_tensor(dev[:, :], dev[:, :], dev[:, :], ALU.mult))
        step(dve.tensor_tensor(dev[:, :], dev[:, :], mv[:, :, 1], ALU.add))
        dve.wait_ge(var_mm, 1)
        step(dve.tensor_scalar(gv[:, :], var_ps, GN_EPS, None, ALU.add))
        dve.wait_ge(a_step, 2)
        step(dve.tensor_tensor(tmp[:, :], scale, scale, ALU.mult))
        step(dve.tensor_tensor(tmp[:, :], tmp[:, :], gv[:, :], ALU.mult))
        step(dve.tensor_scalar(tmp[:, :], tmp[:, :], -0.5, 1.5, ALU.mult, ALU.add))
        step(dve.tensor_tensor(scale, scale, tmp[:, :], ALU.mult))
        dve.scalar_tensor_tensor(bias, gm[:, :], -1.0, scale, ALU.mult, ALU.mult).then_inc(done, 1)

    def tensor(pe):
        pe.wait_ge(v_step, tiles)
        pe.matmul(mean_ps, averages, mv[:, :, 0], start=True, stop=True).then_inc(mean_mm, 1)
        pe.wait_ge(v_step, tiles + 4)
        pe.matmul(var_ps, averages, dev[:, :], start=True, stop=True).then_inc(var_mm, 1)

    def scalar(act):
        act.wait_ge(v_step, tiles + 5)
        act.activation(scale, gv[:, :], ACT.Ln).then_inc(a_step, 1)
        act.wait_ge(a_step, 1)
        act.activation(scale, scale, ACT.Exp, scale=-0.5).then_inc(a_step, 1)

    return vector, tensor, scalar


def mamba_and_linear_attention(nc, x, ln_w, ln_b, in_proj, conv_w, conv_b, x_proj, dt_proj, dt_b, a_log, d_skip,
                               out_proj, qkv, q_rows, w_out1, b_out1, out):
    x_v = x.rearrange("b (ct p) (cb t) -> b cb p ct t", p=P, t=T)
    x2_d = nc.dram_tensor("x2", [BATCH, DIM, TOKENS], FP32).ap()
    x2_v = x2_d.rearrange("b (ct p) (cb t) -> b cb ct p t", p=P, t=T)
    x_tile_v = x.rearrange("b (ct p) (cb t) -> b cb ct p t", p=P, t=T)
    bc_d = nc.dram_tensor("b_and_c_rows", [2 * STATE, T], FP32).ap()

    outer = ExitStack()
    with outer:
        def sb(name, shape, stack=outer, dtype=FP32):
            return stack.enter_context(nc.sbuf_tensor(name, shape, dtype))

        def sem(name):
            return outer.enter_context(nc.semaphore(name))

        identity = sb("identity", [P, P])
        averages = sb("averages", [P, P])
        x2_stats = sb("x2_stats", [P, CT, CHUNKS, 6])

        layer0 = ExitStack()
        with layer0:
            w_in = sb("w_in", [P, CT, 2 * INNER], layer0)
            w_out = sb("w_out", [P, JT, DIM], layer0)
            w_x = sb("w_x", [P, JT, P], layer0)
            w_dt = sb("w_dt", [3 * RANK, INNER], layer0, FP32R)
            w_conv = sb("w_conv", [P, JT, TAPS], layer0)
            b_conv = sb("b_conv", [P, JT], layer0)
            b_dt = sb("b_dt", [P, JT], layer0)
            skip = sb("skip", [P, JT], layer0)
            w_ln = sb("w_ln", [P, CT], layer0)
            b_ln = sb("b_ln", [P, CT], layer0)
            neg_a = sb("neg_a", [P, JT, STATE], layer0)
            channel_mean = sb("channel_mean", [P, P], layer0)
            eps = sb("eps", [P, 1], layer0)
            keep_now = sb("keep_now", [P, 2], layer0)
            one = sb("one", [P, 1], layer0)
            minus_one = sb("minus_one", [P, 1], layer0)
            keep = sb("keep", [P, CHUNKS + 2], layer0)
            gn_scale = sb("gn_scale", [P, BATCH * CT], layer0)
            gn_bias = sb("gn_bias", [P, BATCH * CT], layer0)

            bc = sb("bc", [P, 2, STATE, T], layer0)
            xs = sb("xs", [P, 2, JT, T], layer0)
            xn = sb("xn", [P, 2, CT, T], layer0)
            sq = sb("sq", [P, 2, T], layer0)
            acc = sb("acc", [P, T], layer0)
            zs = sb("zs", [P, T], layer0)
            halo = sb("halo", [P, JT, TAPS - 1], layer0)
            carry = sb("carry", [P, STEPS], layer0)
            sp_e = sb("sp_e", [P, T], layer0)
            sp_w = sb("sp_w", [P, T], layer0)
            sp_l = sb("sp_l", [P, T], layer0)
            sp_m = sb("sp_m", [P, T], layer0)
            delta = sb("delta", [P, 2, T], layer0)
            hs = sb("hs", [P, H_RING, T], layer0)
            hc = sb("hc", [P, HC_RING, T], layer0)
            xres = sb("xres", [P, 2, T], layer0)
            dt_rows = sb("dt_rows", [3 * RANK, T], layer0, FP32R)

            banks = [layer0.enter_context(nc.psum_tensor(f"bank{i}", [P, T], FP32)) for i in range(8)]
            y_ps, da_ps = banks[0], banks[1:4]
            du_ps, pa, pb, pout = banks[4:8]
            out_ps = (pout, pout, pa, pout)
            in_ps = (pa, pout)

            bc_rows = sq[3 * RANK:, 0, :]

            w_in_loaded, w_out_loaded = sem("w_in_loaded"), sem("w_out_loaded")
            weights_in = sem("weights_in")
            xin_stage = [sem(f"x_stage{i}") for i in range(2)]
            stats_done = sem("stats_done")
            consts = sem("consts")
            halved = sem("halved")
            dt_high = sem("dt_high")
            a_exp = sem("a_exp")
            gn_done = sem("gn_done")
            n_weights = 9

            with ExitStack() as setup:
                stage = bc[:, :, :, :].rearrange("p a n t -> p a (n t)")
                w_dt_raw = xs[0:3 * RANK, 0, 0:INNER // T, :].rearrange("p a t -> p (a t)")
                first_stats = sq[:, :, :].rearrange("p a t -> p (a t)")[:, 0:BATCH * CT * CB * 6]
                first_stats = first_stats.rearrange("p (i s) -> p i s", i=BATCH * CT)
                block = setup.enter_context(nc.Block())
                gc_vector, gc_tensor, gc_scalar = group_coefficients(
                    nc, setup, block, "gn0", lambda i: first_stats[:, i, :], BATCH * CT, CB, averages[:, :], pa,
                    gn_scale[:, :], gn_bias[:, :])

                @block.sync
                def _(sp):
                    x_rows = x.rearrange("b (ct p) l -> (b ct) p l", p=P)
                    sp.dma_start(w_in[:, :, :], in_proj.rearrange("(ct p) n -> p ct n", p=P)).then_inc(w_in_loaded, 16)
                    sp.dma_start(w_x[:, :, :], x_proj.rearrange("(j p) n -> p j n", p=P)).then_inc(weights_in, 16)
                    sp.dma_start(w_dt_raw, dt_proj).then_inc(weights_in, 16)
                    sp.dma_start(w_conv[:, :, :], conv_w).then_inc(weights_in, 16)
                    sp.dma_start(b_conv[:, :], conv_b).then_inc(weights_in, 16)
                    sp.dma_start(b_dt[:, :], dt_b).then_inc(weights_in, 16)
                    sp.dma_start(skip[:, :], d_skip).then_inc(weights_in, 16)
                    sp.dma_start(w_ln[:, :], ln_w).then_inc(weights_in, 16)
                    sp.dma_start(b_ln[:, :], ln_b).then_inc(weights_in, 16)
                    sp.dma_start(neg_a[:, :, :], a_log).then_inc(weights_in, 16)
                    for i in range(BATCH * CT):
                        wait(sp, stats_done, CB * (i - 1))
                        sp.dma_start(stage[:, i % 2, 0:TOKENS], x_rows[i]).then_inc(xin_stage[i % 2], 16)
                    sp.dma_start(w_out[:, :, :], out_proj.rearrange("(j p) n -> p j n", p=P)).then_inc(w_out_loaded, 16)

                @block.gpsimd
                def _(pool):
                    pool.memset(identity[:, :], 1.0).then_inc(consts, 1)
                    pool.memset(averages[:, :], 1.0 / GROUP).then_inc(consts, 1)
                    pool.memset(channel_mean[:, :], 1.0 / DIM).then_inc(consts, 1)
                    pool.memset(keep[:, :], 1.0).then_inc(consts, 1)
                    pool.memset(halo[:, :, :], 0.0).then_inc(consts, 1)
                    pool.memset(carry[:, :], 0.0).then_inc(consts, 1)
                    pool.memset(eps[:, :], LN_EPS).then_inc(consts, 1)
                    pool.memset(one[:, :], 1.0).then_inc(consts, 1)
                    pool.memset(minus_one[:, :], -1.0).then_inc(consts, 1)
                    pool.wait_ge(consts, 9)
                    pool.affine_select(out=identity[:, :], in_=identity[:, :], compare_op=ALU.is_equal, fill=0.0,
                                       base=0, pattern=[[-1, P]], channel_multiplier=1).then_inc(consts, 1)
                    groups = averages[:, :].rearrange("p (a g) -> p a g", g=GROUP)
                    pool.affine_select(out=groups, in_=groups, compare_op=ALU.is_ge, fill=0.0, base=0,
                                       pattern=[[-GROUP, P // GROUP], [0, GROUP]],
                                       channel_multiplier=1).then_inc(consts, 1)
                    pool.memset(keep[:, CB:CB + 1], 0.0).then_inc(consts, 1)
                    pool.wait_ge(consts, 12)
                    pool.affine_select(out=groups, in_=groups, compare_op=ALU.is_ge, fill=0.0, base=GROUP - 1,
                                       pattern=[[GROUP, P // GROUP], [0, GROUP]],
                                       channel_multiplier=-1).then_inc(consts, 1)
                    pool.wait_ge(w_in_loaded, 16)
                    pool.tensor_scalar(w_in[:, :, INNER:], w_in[:, :, INNER:], 0.5, None, ALU.mult).then_inc(halved, 1)
                    pool.wait_ge(weights_in, 16 * n_weights)
                    pool.tensor_scalar(w_conv[:, :, :], w_conv[:, :, :], 0.5, None, ALU.mult).then_inc(halved, 1)
                    pool.tensor_scalar(b_conv[:, :], b_conv[:, :], 0.5, None, ALU.mult).then_inc(halved, 1)
                    pool.tensor_copy(w_dt[:, :], w_dt_raw).then_inc(dt_high, 1)
                    pool.wait_ge(dt_high, 1)
                    low = slice(2 * RANK, 3 * RANK)
                    pool.tensor_tensor(w_dt[low, :], w_dt_raw[low, :], w_dt[low, :], ALU.subtract).then_inc(halved, 1)
                    pool.wait_ge(halved, 4)
                    pool.wait_ge(a_exp, 1)
                    pool.tensor_scalar(neg_a[:, :, :], neg_a[:, :, :], -1.0, None, ALU.mult).then_inc(halved, 1)

                @block.vector
                def _(dve):
                    for i in range(BATCH * CT):
                        dve.wait_ge(xin_stage[i % 2], 16 * (i // 2 + 1))
                        for k in range(CB):
                            dve.bn_stats(first_stats[:, i, 6 * k:6 * k + 6],
                                         stage[:, i % 2, k * T:(k + 1) * T]).then_inc(stats_done, 1)
                    dve.wait_ge(stats_done, BATCH * CT * CB)
                    gc_vector(dve, gn_done)

                @block.tensor
                def _(pe):
                    pe.wait_ge(consts, 13)
                    gc_tensor(pe)

                @block.scalar
                def _(act):
                    act.wait_ge(weights_in, 16 * n_weights)
                    act.activation(neg_a[:, :, :], neg_a[:, :, :], ACT.Exp).then_inc(a_exp, 1)
                    gc_scalar(act)

            sp_fence, act_fence = sem("sp_fence"), sem("act_fence")
            keep_set, carried = sem("keep_set"), sem("carried")
            x_loaded = sem("x_loaded")
            gn_applied = sem("gn_applied")
            mean_mm = sem("mean_mm")
            centered = sem("centered")
            squared = sem("squared")
            var_mm = sem("var_mm")
            rstd_guess = sem("rstd_guess")
            newton = sem("newton")
            scaled = sem("scaled")
            xn_ready = sem("xn_ready")
            in_mm = sem("in_mm")
            tap3 = sem("tap3")
            conv_step = sem("conv_step")
            halo_saved = sem("halo_saved")
            tanh_x = sem("tanh_x")
            xs_ready = sem("xs_ready")
            x_mm = sem("x_mm")
            dt_split = sem("dt_split")
            dbl_ready = sem("dbl_ready")
            bc_stored = sem("bc_stored")
            bc_loaded = [sem(f"bc_loaded{n}") for n in range(STATE)]
            dt_mm = sem("dt_mm")
            dt_read = sem("dt_read")
            sp_exp = sem("sp_exp")
            sp_step = sem("sp_step")
            sp_rest = sem("sp_rest")
            sp_ln = sem("sp_ln")
            sp_sum = sem("sp_sum")
            delta_ready = sem("delta_ready")
            z_mm = sem("z_mm")
            tanh_z = sem("tanh_z")
            zs_ready = sem("zs_ready")
            du_ready = sem("du_ready")
            da_ready = sem("da_ready")
            dbu_ready = sem("dbu_ready")
            h_ready = sem("h_ready")
            hc_ready = sem("hc_ready")
            n_summed = sem("n_summed")
            y_skip = sem("y_skip")
            gated = sem("gated")
            out_mm = sem("out_mm")
            res_loaded = [sem(f"res_loaded{i}") for i in range(2)]
            x2_ready = sem("x2_ready")
            x2_stat = sem("x2_stat")
            x2_stored = [sem(f"x2_stored{i}") for i in range(2)]

            def settle(engine, fence):
                engine.sem_inc(fence, 1)

            def chunk_loop(body):
                def on(engine):
                    body(engine, -1, False, True, False)
                    body(engine, 0, True, True, False)
                    with engine.Fori(1, CHUNKS - 1) as c:
                        body(engine, c, True, True, True)
                    body(engine, CHUNKS - 1, True, False, True)
                    body(engine, CHUNKS, False, False, True)
                return on

            with ExitStack() as main:
                block = main.enter_context(nc.Block())

                def sync_chunk(sp, c, scan, front, project):
                    f = c + 1
                    if project:
                        o = c - 1
                        for ct in range(CT + 2):
                            if ct < CT:
                                sp.wait_ge(x2_stored[ct % 2], 16 * (2 * o + ct // 2 + 1))
                                settle(sp, sp_fence)
                                sp.dma_start(xres[:, ct % 2, :],
                                             x_tile_v[o // CB, o % CB, ct]).then_inc(res_loaded[ct % 2], 16)
                            if ct >= 1 and ct - 1 < CT:
                                k = ct - 1
                                sp.wait_ge(x2_stat, CT * o + k + 1)
                                settle(sp, sp_fence)
                                sp.dma_start(x2_v[o // CB, o % CB, k],
                                             xres[:, k % 2, :]).then_inc(x2_stored[k % 2], 16)
                    if front:
                        wait(sp, dbu_ready, STEPS * c + STATE + 1)
                        settle(sp, sp_fence)
                        sp.wait_ge(dbl_ready, f + 1)
                        sp.dma_start(bc_d, bc_rows).then_inc(bc_stored, 16)
                        sp.wait_ge(bc_stored, 16 * (f + 1))
                        settle(sp, sp_fence)
                        for n in range(STATE):
                            wait(sp, dbu_ready, STEPS * c + (JT - 1) * STATE + n + 1)
                            wait(sp, hc_ready, STEPS * c + (JT - 1) * STATE + n + 1)
                            for k in range(2):
                                row = STATE * k + n
                                sp.dma_start(bc[:, k, n, :],
                                             bc_d[row:row + 1, :].partition_broadcast(P)).then_inc(bc_loaded[n], 16)

                def scalar_chunk(act, c, scan, front, project):
                    f = c + 1
                    for j in range(JT):
                        for n in range(STATE):
                            tile, slot = JT * c + j, STATE * j + n
                            step = STEPS * c + slot
                            if front and slot == 0:
                                wait(act, z_mm, JT * c)
                                settle(act, act_fence)
                                act.dma_start(xn[:, f % 2, :, :], x_v[f // CB, f % CB]).then_inc(x_loaded, 16)
                            if front and slot in NORM:
                                ct = NORM.index(slot)
                                if ct == 0:
                                    act.wait_ge(x_loaded, 16 * (f + 1))
                                    settle(act, act_fence)
                                k = (f // CB) * CT + ct
                                act.activation(xn[:, f % 2, ct, :], xn[:, f % 2, ct, :], ACT.Identity,
                                               scale=gn_scale[:, bass.ds(k, 1)],
                                               bias=gn_bias[:, bass.ds(k, 1)]).then_inc(gn_applied, 1)
                            if front and slot in SQUARE:
                                if slot == SQUARE[0]:
                                    act.wait_ge(centered, f + 1)
                                for ct in ((0, 1) if slot == SQUARE[0] else (2, 3)):
                                    wait(act, bc_stored, 16 * f)
                                    wait(act, var_mm, CT * f + ct - 1)
                                    wait(act, scaled, f)
                                    settle(act, act_fence)
                                    act.activation(sq[:, ct % 2, :], xn[:, f % 2, ct, :],
                                                   ACT.Square).then_inc(squared, 1)
                            if front and slot == RSTD:
                                act.wait_ge(var_mm, CT * (f + 1))
                                act.activation(sq[:, 0, :], pa[:, :], ACT.Ln, bias=eps[:, 0:1]).then_inc(rstd_guess, 1)
                                act.wait_ge(rstd_guess, 2 * f + 1)
                                act.activation(sq[:, 0, :], sq[:, 0, :], ACT.Exp,
                                               scale=-0.5).then_inc(rstd_guess, 1)
                            if front and AFFINE <= slot < AFFINE + CT:
                                ct = slot - AFFINE
                                if ct == 0:
                                    act.wait_ge(scaled, f + 1)
                                    settle(act, act_fence)
                                act.activation(xn[:, f % 2, ct, :], xn[:, f % 2, ct, :], ACT.Identity,
                                               scale=w_ln[:, ct:ct + 1],
                                               bias=b_ln[:, ct:ct + 1]).then_inc(xn_ready, 1)
                            for t in range(JT) if front else ():
                                if slot == IN_MM[t] + TAP3:
                                    act.wait_ge(in_mm, JT * f + t + 1)
                                    wait(act, xs_ready, JT * f + t)
                                    act.activation(acc[:, :], in_ps[t % 2][:, :], ACT.Identity,
                                                   scale=w_conv[:, t, TAPS - 1:TAPS],
                                                   bias=b_conv[:, t:t + 1]).then_inc(tap3, 1)
                                if slot == IN_MM[t] + TANH:
                                    act.wait_ge(conv_step, 6 * (JT * f + t + 1))
                                    act.activation(halo[:, t, :], in_ps[t % 2][:, T - 3:T], ACT.Copy,
                                                   scale=keep_now[:, 1:2]).then_inc(halo_saved, 1)
                                    wait(act, out_mm, CT * c)
                                    settle(act, act_fence)
                                    act.activation(xs[:, f % 2, t, :], acc[:, :], ACT.Tanh).then_inc(tanh_x, 1)
                            if front and slot == DBL:
                                act.wait_ge(x_mm, f + 1)
                                wait(act, dt_mm, JT * f)
                                wait(act, bc_stored, 16 * f)
                                act.activation(bc_rows, pa[3 * RANK:, :], ACT.Copy)
                                act.activation(dt_rows[:, :], pa[0:3 * RANK, :], ACT.Copy).then_inc(dbl_ready, 1)
                            if front if j == 7 else scan:
                                nt = tile + 1
                                dt_ps = pout if j == 7 else pb
                                jn = (j + 1) % JT
                                if n == (SP_ABS7 if j == 7 else SP_ABS):
                                    act.wait_ge(dt_mm, nt + 1)
                                    wait(act, delta_ready, nt)
                                    act.activation(sp_e[:, :], dt_ps[:, :], ACT.Abs,
                                                   bias=b_dt[:, jn:jn + 1]).then_inc(sp_exp, 1)
                                    act.activation(sp_m[:, :], dt_ps[:, :], ACT.Relu,
                                                   bias=b_dt[:, jn:jn + 1]).then_inc(dt_read, 1)
                                if n == (SP_EXP7 if j == 7 else SP_EXP):
                                    act.wait_ge(sp_exp, 2 * nt + 1)
                                    act.activation(sp_e[:, :], sp_e[:, :], ACT.Exp, scale=-1.0).then_inc(sp_exp, 1)
                                    act.wait_ge(sp_exp, 2 * nt + 2)
                                    act.activation(sp_w[:, :], sp_e[:, :], ACT.Identity,
                                                   bias=one[:, 0:1]).then_inc(sp_step, 1)
                                if n == (SP_ROUND7 if j == 7 else SP_ROUND):
                                    act.wait_ge(sp_step, 2 * nt + 1)
                                    act.activation(sp_w[:, :], sp_w[:, :], ACT.Identity,
                                                   bias=minus_one[:, 0:1]).then_inc(sp_step, 1)
                                if n == (SP_LN7 if j == 7 else SP_LN):
                                    act.activation(sp_l[:, :], sp_e[:, :], ACT.Ln, bias=one[:, 0:1]).then_inc(sp_ln, 1)
                            if scan and n == Z_TANH:
                                act.wait_ge(z_mm, tile + 1)
                                wait(act, gated, tile)
                                act.activation(zs[:, :], pb[:, :], ACT.Tanh).then_inc(tanh_z, 1)
                            if scan and n > 0 or (j > 0 and scan):
                                prev = step - 1
                                col = STATE * j + n - 1
                                act.wait_ge(h_ready, prev + 1)
                                act.activation(carry[:, col:col + 1], hs[:, (n - 1) % H_RING, T - 1:T], ACT.Copy,
                                               scale=keep_now[:, 0:1]).then_inc(carried, 1)
                            if scan and j == 0 and n == 0 and not (isinstance(c, int) and c == 0):
                                act.wait_ge(h_ready, step)
                                act.activation(carry[:, STEPS - 1:STEPS], hs[:, H_RING - 1, T - 1:T], ACT.Copy,
                                               scale=keep_now[:, 0:1]).then_inc(carried, 1)
                            if (scan or front) and j == 0 and n == 0:
                                wait(act, carried, STEPS * c)
                                wait(act, halo_saved, JT * f)
                                act.activation(keep_now[:, :], keep[:, bass.ds(c + 1, 2)], ACT.Copy).then_inc(keep_set, 1)
                                act.wait_ge(keep_set, c + 2)
                            target = slot + 2
                            if scan if target < STEPS else front:
                                jn, nn = target // STATE % JT, target % STATE
                                if nn == 0:
                                    act.wait_ge(delta_ready, tile + 2)
                                wait(act, h_ready, step + (target % STEPS < DA_RING - 1))
                                act.activation(da_ps[target % STEPS % DA_RING][:, :], delta[:, jn % 2, :], ACT.Exp,
                                               scale=neg_a[:, jn, nn:nn + 1]).then_inc(da_ready, 1)

                def vector_chunk(dve, c, scan, front, project):
                    f = c + 1
                    for j in range(JT):
                        for n in range(STATE):
                            tile, slot = JT * c + j, STATE * j + n
                            step = STEPS * c + slot
                            if front and slot == CENTER:
                                dve.wait_ge(mean_mm, f + 1)
                                dve.tensor_tensor(xn[:, f % 2, :, :], xn[:, f % 2, :, :],
                                                  pa[:, :].unsqueeze(1).broadcast_to([P, CT, T]),
                                                  ALU.subtract).then_inc(centered, 1)
                            if front and slot == NEWTON:
                                dve.wait_ge(rstd_guess, 2 * f + 2)
                                dve.tensor_tensor(sq[:, 1, :], sq[:, 0, :], sq[:, 0, :], ALU.mult).then_inc(newton, 1)
                                dve.wait_ge(newton, 4 * f + 1)
                                dve.scalar_tensor_tensor(sq[:, 1, :], pa[:, :], LN_EPS, sq[:, 1, :], ALU.add,
                                                         ALU.mult).then_inc(newton, 1)
                                dve.wait_ge(newton, 4 * f + 2)
                                dve.tensor_scalar(sq[:, 1, :], sq[:, 1, :], -0.5, 1.5, ALU.mult,
                                                  ALU.add).then_inc(newton, 1)
                                dve.wait_ge(newton, 4 * f + 3)
                                dve.tensor_tensor(sq[:, 0, :], sq[:, 0, :], sq[:, 1, :], ALU.mult).then_inc(newton, 1)
                            if front and slot == SCALE:
                                dve.wait_ge(newton, 4 * f + 4)
                                dve.tensor_tensor(xn[:, f % 2, :, :], xn[:, f % 2, :, :],
                                                  sq[:, 0:1, :].broadcast_to([P, CT, T]),
                                                  ALU.mult).then_inc(scaled, 1)
                            for t in range(JT) if front else ():
                                if slot == IN_MM[t] + CONV:
                                    dve.wait_ge(tap3, JT * f + t + 1)
                                    wait(dve, halo_saved, JT * (f - 1) + t + 1)
                                    k = 6 * (JT * f + t)
                                    for s in range(1, TAPS):
                                        wait(dve, conv_step, k + 2 * (s - 1))
                                        w = w_conv[:, t, TAPS - 1 - s:TAPS - s]
                                        dve.scalar_tensor_tensor(acc[:, s:T], in_ps[t % 2][:, 0:T - s], w, acc[:, s:T], ALU.mult,
                                                                 ALU.add).then_inc(conv_step, 1)
                                        dve.scalar_tensor_tensor(acc[:, 0:s], halo[:, t, TAPS - 1 - s:TAPS - 1], w,
                                                                 acc[:, 0:s], ALU.mult,
                                                                 ALU.add).then_inc(conv_step, 1)
                                if slot == IN_MM[t] + SILU:
                                    dve.wait_ge(tanh_x, JT * f + t + 1)
                                    half = xs[:, f % 2, t, :]
                                    dve.scalar_tensor_tensor(half, half, 1.0, acc[:, :], ALU.add,
                                                             ALU.mult).then_inc(xs_ready, 1)
                            if front and slot == DT_SPLIT:
                                dve.wait_ge(dbl_ready, f + 1)
                                mid = slice(RANK, 2 * RANK)
                                dve.tensor_tensor(dt_rows[mid, :], pa[mid, :], dt_rows[mid, :],
                                                  ALU.subtract).then_inc(dt_split, 1)
                            if scan and n == Z_SILU:
                                dve.wait_ge(tanh_z, tile + 1)
                                dve.scalar_tensor_tensor(zs[:, :], zs[:, :], 1.0, pb[:, :], ALU.add,
                                                         ALU.mult).then_inc(zs_ready, 1)
                            if n == Y_SKIP and ((scan and j > 0) or (project and j == 0)):
                                jp, o = (j - 1) % JT, (c if j > 0 else c - 1)
                                dve.wait_ge(n_summed, STATE * tile)
                                dve.scalar_tensor_tensor(xs[:, o % 2, jp, :], xs[:, o % 2, jp, :], skip[:, jp:jp + 1],
                                                         y_ps[:, :], ALU.mult, ALU.add).then_inc(y_skip, 1)
                            if project and slot in OUT_ADD:
                                ct = OUT_ADD.index(slot)
                                o = c - 1
                                dve.wait_ge(out_mm, CT * o + ct + 1)
                                dve.wait_ge(res_loaded[ct % 2], 16 * (2 * o + ct // 2 + 1))
                                dve.tensor_tensor(xres[:, ct % 2, :], out_ps[ct][:, :], xres[:, ct % 2, :],
                                                  ALU.add).then_inc(x2_ready, 1)
                                dve.wait_ge(x2_ready, CT * o + ct + 1)
                                dve.bn_stats(x2_stats[:, ct, bass.ds(o, 1), :].rearrange("p a s -> p (a s)"),
                                             xres[:, ct % 2, :]).then_inc(x2_stat, 1)
                            last = j == JT - 1 and n == STATE - 1
                            if (scan and not last) or (last and front):
                                nn, jn = (n + 1) % STATE, (j + (n + 1) // STATE) % JT
                                cn = c + 1 if last else c
                                if nn == 0:
                                    wait(dve, dbu_ready, step + 1)
                                    dve.wait_ge(delta_ready, tile + 2)
                                    wait(dve, xs_ready, JT * cn + jn + 1)
                                    dve.tensor_tensor(du_ps[:, :], delta[:, jn % 2, :], xs[:, cn % 2, jn, :],
                                                      ALU.mult).then_inc(du_ready, 1)
                                    dve.wait_ge(du_ready, tile + 2)
                                if jn == 0:
                                    dve.wait_ge(bc_loaded[nn], 32 * (cn + 1))
                                wait(dve, hc_ready, step + 2 - H_RING)
                                wait(dve, carried, step + 2 - H_RING)
                                dve.tensor_tensor(hs[:, nn % H_RING, :], du_ps[:, :], bc[:, 0, nn, :],
                                                  ALU.mult).then_inc(dbu_ready, 1)
                            if scan:
                                dve.wait_ge(da_ready, step + 1)
                                dve.wait_ge(dbu_ready, step + 1)
                                dve.tensor_tensor_scan(hs[:, n % H_RING, :], da_ps[slot % DA_RING][:, :],
                                                       hs[:, n % H_RING, :],
                                                       carry[:, STATE * j + n:STATE * j + n + 1], ALU.mult,
                                                       ALU.add).then_inc(h_ready, 1)

                def gpsimd_chunk(pool, c, scan, front, project):
                    for j in range(JT):
                        for n in range(STATE):
                            tile, slot = JT * c + j, STATE * j + n
                            step = STEPS * c + slot
                            if (front if j == 7 else scan) and n == (SP_REST7 if j == 7 else SP_REST):
                                pool.wait_ge(sp_step, 2 * tile + 4)
                                pool.tensor_tensor(sp_w[:, :], sp_w[:, :], sp_e[:, :], ALU.subtract).then_inc(sp_rest, 1)
                            nt = tile + 1
                            if (front if j == 7 else scan) and n == (SP_SUM7 if j == 7 else SP_SUM):
                                pool.wait_ge(sp_ln, nt + 1)
                                pool.tensor_tensor(sp_m[:, :], sp_m[:, :], sp_l[:, :], ALU.add).then_inc(sp_sum, 1)
                            if (front if j == 7 else scan) and n == (SP_DELTA7 if j == 7 else SP_DELTA):
                                pool.wait_ge(sp_sum, nt + 1)
                                pool.wait_ge(sp_rest, nt + 1)
                                wait(pool, da_ready, STATE * (nt - 1))
                                wait(pool, du_ready, nt - 1)
                                pool.tensor_tensor(delta[:, (j + 1) % 2, :], sp_m[:, :], sp_w[:, :],
                                                   ALU.subtract).then_inc(delta_ready, 1)
                            if n == Y_GATE and ((scan and j > 0) or (project and j == 0)):
                                jp, o = (j - 1) % JT, (c if j > 0 else c - 1)
                                pool.wait_ge(y_skip, tile)
                                pool.wait_ge(zs_ready, tile)
                                pool.tensor_tensor(xs[:, o % 2, jp, :], xs[:, o % 2, jp, :], zs[:, :],
                                                   ALU.mult).then_inc(gated, 1)
                            if scan:
                                pool.wait_ge(h_ready, step + 1)
                                wait(pool, n_summed, step + 1 - HC_RING)
                                pool.tensor_tensor(hc[:, n % HC_RING, :], hs[:, n % H_RING, :], bc[:, 1, n, :],
                                                   ALU.mult).then_inc(hc_ready, 1)

                def tensor_chunk(pe, c, scan, front, project):
                    f = c + 1
                    for j in range(JT):
                        for n in range(STATE):
                            tile, slot = JT * c + j, STATE * j + n
                            step = STEPS * c + slot
                            if front and slot in MEAN:
                                ct = MEAN.index(slot)
                                pe.wait_ge(gn_applied, CT * f + ct + 1)
                                if ct == 0:
                                    wait(pe, dt_split, f)
                                mm = pe.matmul(pa[:, :], channel_mean[:, :], xn[:, f % 2, ct, :], start=ct == 0,
                                               stop=ct == CT - 1)
                                if ct == CT - 1:
                                    mm.then_inc(mean_mm, 1)
                            if front and slot in VARIANCE:
                                ct = VARIANCE.index(slot)
                                pe.wait_ge(squared, CT * f + ct + 1)
                                pe.matmul(pa[:, :], channel_mean[:, :], sq[:, ct % 2, :], start=ct == 0,
                                          stop=ct == CT - 1).then_inc(var_mm, 1)
                            for t in range(JT) if front else ():
                                ct = slot - IN_MM[t]
                                if not 0 <= ct < CT:
                                    continue
                                if ct == 0 and t < 2:
                                    pe.wait_ge(xn_ready, CT * (f + 1))
                                    wait(pe, x2_ready, CT * (c - 1) + 3 + t)
                                    if not project:
                                        pe.wait_ge(newton, 4 * f + 2)
                                elif ct == 0:
                                    pe.wait_ge(halo_saved, JT * f + t - 1)
                                mm = pe.matmul(in_ps[t % 2][:, :], w_in[:, ct, t * P:(t + 1) * P], xn[:, f % 2, ct, :],
                                               start=ct == 0, stop=ct == CT - 1)
                                if ct == CT - 1:
                                    mm.then_inc(in_mm, 1)
                            if front and slot in X_MM:
                                k = X_MM.index(slot)
                                if k == 0:
                                    pe.wait_ge(halo_saved, JT * (f + 1) - 1)
                                for t in (2 * k, 2 * k + 1):
                                    pe.wait_ge(xs_ready, JT * f + t + 1)
                                    mm = pe.matmul(pa[:, :], w_x[:, t, :], xs[:, f % 2, t, :], start=t == 0,
                                                   stop=t == JT - 1)
                                if k == 3:
                                    mm.then_inc(x_mm, 1)
                            if n == DT_MM and (scan and j < 6 or front and j == 7):
                                wait(pe, zs_ready, tile + 1 if scan else 0)
                                jd = (j + 2) % JT
                                pe.matmul(pb[:, :], w_dt[:, jd * P:(jd + 1) * P], dt_rows[:, :], start=True,
                                          stop=True).then_inc(dt_mm, 1)
                            if front and j == 7 and n == DT_MM7:
                                pe.wait_ge(dt_split, f + 1)
                                pe.wait_ge(halo_saved, JT * (f + 1))
                                pe.matmul(pout[:, :], w_dt[:, 0:P], dt_rows[:, :], start=True,
                                          stop=True).then_inc(dt_mm, 1)
                            for ct in range(CT) if scan else ():
                                if n != Z_MM[ct]:
                                    continue
                                if ct == 0:
                                    pe.wait_ge(dt_read, tile + 1 + (j < 7))
                                    wait(pe, zs_ready, tile)
                                lo = INNER + j * P
                                mm = pe.matmul(pb[:, :], w_in[:, ct, lo:lo + P], xn[:, c % 2, ct, :], start=ct == 0,
                                               stop=ct == CT - 1)
                                if ct == CT - 1:
                                    mm.then_inc(z_mm, 1)
                            for ct in range(CT) if project else ():
                                if slot not in OUT_MM[ct]:
                                    continue
                                k, o = OUT_MM[ct].index(slot), c - 1
                                if ct == 0:
                                    pe.wait_ge(gated, JT * (c - 1) + k + 1)
                                if k == 0 and ct == 0 and scan:
                                    pe.wait_ge(dt_read, JT * c + 1)
                                elif k == 0 and ct in (1, 3):
                                    pe.wait_ge(x2_ready, CT * o + ct - ct // 3)
                                elif k == 0 and ct == 2 and front:
                                    pe.wait_ge(newton, 4 * f + 2)
                                mm = pe.matmul(out_ps[ct][:, :], w_out[:, k, ct * P:(ct + 1) * P], xs[:, o % 2, k, :],
                                               start=k == 0, stop=k == JT - 1)
                                if k == JT - 1:
                                    mm.then_inc(out_mm, 1)
                            if (scan and slot >= SUM_LAG) or (project and slot < SUM_LAG):
                                js, ns = (slot - SUM_LAG) // STATE % JT, (slot - SUM_LAG) % STATE
                                pe.wait_ge(hc_ready, step - SUM_LAG + 1)
                                if ns == 0:
                                    wait(pe, y_skip, tile)
                                pe.matmul(y_ps[:, :], identity[:, :], hc[:, ns % HC_RING, :], start=ns == 0,
                                          stop=ns == STATE - 1).then_inc(n_summed, 1)

                @block.sync
                def _(sp):
                    for i in range(2):
                        sp.sem_inc(x2_stored[i], 16)
                    chunk_loop(sync_chunk)(sp)
                    for i in range(2):
                        sp.wait_ge(x2_stored[i], 16 * (CHUNKS * CT // 2 + 1))

                @block.scalar
                def _(act):
                    chunk_loop(scalar_chunk)(act)

                @block.vector
                def _(dve):
                    chunk_loop(vector_chunk)(dve)

                @block.gpsimd
                def _(pool):
                    chunk_loop(gpsimd_chunk)(pool)

                @block.tensor
                def _(pe):
                    pe.wait_ge(w_out_loaded, 16)
                    chunk_loop(tensor_chunk)(pe)

        layer1 = ExitStack()
        with layer1:
            w_k = [sb(f"w_k_{part}", [P, CT, DIM], layer1, FP32R) for part in ("high", "low")]
            w_v = [sb(f"w_v_{part}", [P, CT, DIM], layer1, FP32R) for part in ("high", "low")]
            w_q = sb("w_q", [P, CT, DIM], layer1)
            w_o = sb("w_o", [P, CT, DIM], layer1)
            b_o = sb("b_o", [P, CT], layer1)
            gn1_scale = sb("gn1_scale", [P, BATCH * CT], layer1)
            gn1_bias = sb("gn1_bias", [P, BATCH * CT], layer1)
            keys = sb("keys", [P, CT, TOKENS], layer1)
            xl = sb("xl", [P, 2, CT, T], layer1)
            xg = sb("xg", [P, 2, T], layer1)
            xg_parts = [sb(f"xg_{part}", [P, 2, CT, T], layer1, FP32R) for part in ("high", "low")]
            ek = sb("ek", [P, 2, CT, T], layer1)
            v_t = sb("v_t", [P, 2, DIM], layer1)
            ek_t = sb("ek_t", [P, 2, DIM], layer1)
            key_max = sb("key_max", [P, CT, CB], layer1)
            neg_max = sb("neg_max", [P, CT], layer1)
            key_sum = sb("key_sum", [P, CT, CB], layer1)
            inv_sum = sb("inv_sum", [P, CT], layer1)
            context = sb("context", [P, CT, P], layer1)
            g_sb = sb("g_sb", [P, CT, DIM], layer1)
            m_sb = [sb(f"m_{part}", [P, CT, DIM], layer1, FP32R) for part in ("high", "low")]
            banks = [layer1.enter_context(nc.psum_tensor(f"l1_bank{i}", [P, T], FP32)) for i in range(8)]

            w1_loaded, w1_rest_loaded = sem("w1_loaded"), sem("w1_rest_loaded")
            gn1_done, zeroed = sem("gn1_done"), sem("zeroed")
            loaded = [sem(f"loaded{u}") for u in range(2)]
            stored = [sem(f"stored{u}") for u in range(2)]
            normed, lowered = sem("normed"), sem("lowered")
            k_high, k_split, v_split = sem("k_high"), sem("k_split"), sem("v_split")
            m_high = sem("m_high")
            xg_used = sem("xg_used")
            k_mm, k_copied, k_maxed = sem("k_mm"), sem("k_copied"), sem("k_maxed")
            max_step, max_ready = sem("max_step"), sem("max_ready")
            exp_done = sem("exp_done")
            v_mm, v_copied = sem("v_mm"), sem("v_copied")
            tr_mm, ek_copied = sem("tr_mm"), sem("ek_copied")
            ctx_mm, ctx_copied = sem("ctx_mm"), sem("ctx_copied")
            sum_step = sem("sum_step")
            g_mm, g_ready = sem("g_mm"), sem("g_ready")
            m_mm, m_ready = sem("m_mm"), sem("m_ready")
            y_mm, y_ready = sem("y_mm"), sem("y_ready")
            sp1_fence, dve_fence = sem("sp1_fence"), sem("dve_fence")

            PAIRS = CB // 2
            KEYS, VALUES, OUTPUT = range(3)
            out_v = out.rearrange("b (ct p) (cb t) -> b cb p ct t", p=P, t=T)

            def pass_loop(pair, b, number):
                def on(engine):
                    pair(engine, b, number, 0)
                    with engine.Fori(1, PAIRS - 1) as i:
                        pair(engine, b, number, i)
                    pair(engine, b, number, PAIRS - 1)
                return on

            def y_out(u):
                return keys[:, :, u * T:(u + 1) * T]

            def products(pe, out, left, right):
                pairs = ((0, 0), (0, 1), (1, 0))
                for ct in range(CT):
                    for number, (l, r) in enumerate(pairs):
                        last = ct == CT - 1 and number == len(pairs) - 1
                        mm = pe.matmul(out, left(l, ct), right(r, ct), start=ct == 0 and number == 0, stop=last)
                return mm

            with ExitStack() as stack:
                block = stack.enter_context(nc.Block())
                gc_vector, gc_tensor, gc_scalar = group_coefficients(
                    nc, stack, block, "gn1",
                    lambda i: x2_stats[:, i % CT, (i // CT) * CB:(i // CT + 1) * CB, :].rearrange("p c s -> p (c s)"),
                    BATCH * CT, CB, averages[:, :], banks[0], gn1_scale[:, :], gn1_bias[:, :])

                @block.sync
                def _(sp):
                    def load(b, cb, u):
                        sp.dma_start(xl[:, u, :, :], x2_d[b].rearrange("(ct p) (cb t) -> cb p ct t", p=P, t=T)[cb]
                                     ).then_inc(loaded[u], 16)

                    load(0, 0, 0)
                    sp.dma_start(ek[:, 0, :, :], qkv[:, DIM:2 * DIM].rearrange("(ct p) n -> p ct n", p=P)
                                 ).then_inc(w1_loaded, 16)

                    def load_rest():
                        sp.dma_start(ek[:, 1, :, :], qkv[:, 2 * DIM:].rearrange("(ct p) n -> p ct n", p=P)
                                     ).then_inc(w1_rest_loaded, 16)
                        sp.dma_start(w_q[:, :, :], q_rows.rearrange("(m p) n -> p m n", p=P)
                                     ).then_inc(w1_rest_loaded, 16)
                        sp.dma_start(w_o[:, :, :], w_out1.rearrange("(m p) n -> p m n", p=P)
                                     ).then_inc(w1_rest_loaded, 16)
                        sp.dma_start(b_o[:, :], b_out1).then_inc(w1_rest_loaded, 16)

                    def pair(sp, b, number, i):
                        for u in range(2):
                            a, q = CB * b + 2 * i + u, 3 * CB * b + CB * number + 2 * i + u
                            same = not (isinstance(i, int) and i == PAIRS - 1 and u == 1)
                            nb, ncb = (b, 2 * i + u + 1) if same else (b + (number == OUTPUT), 0)
                            if nb < BATCH:
                                wait(sp, normed, CT * q)
                                if number == OUTPUT and not (isinstance(i, int) and i == 0 and u == 0):
                                    settle(sp, sp1_fence)
                                    sp.wait_ge(y_ready, CT * a)
                                settle(sp, sp1_fence)
                                load(nb, ncb, 1 - u)
                            if number == OUTPUT:
                                sp.wait_ge(y_ready, CT * (a + 1))
                                settle(sp, sp1_fence)
                                sp.dma_start(out_v[b, 2 * i + u], y_out(u)).then_inc(stored[u], 16)
                        if b == 0 and number == KEYS and isinstance(i, int) and i == 0:
                            load_rest()

                    for b in range(BATCH):
                        for number in (KEYS, VALUES, OUTPUT):
                            pass_loop(pair, b, number)(sp)
                    for u in range(2):
                        sp.wait_ge(stored[u], 16 * BATCH * PAIRS)

                @block.gpsimd
                def _(pool):
                    pool.memset(context[:, :, :], 0.0).then_inc(zeroed, 1)

                    def pair(pool, b, number, i):
                        for u in range(2):
                            q = 3 * CB * b + CB * number + 2 * i + u
                            for ct in range(CT):
                                pool.wait_ge(normed, CT * q + ct + 1)
                                pool.tensor_tensor(xg_parts[1][:, u, ct, :], xg[:, ct % 2, :],
                                                   xg_parts[0][:, u, ct, :], ALU.subtract).then_inc(lowered, 1)
                        if b == 0 and number == KEYS and isinstance(i, int) and i == 0:
                            pool.wait_ge(w1_rest_loaded, 64)
                            pool.tensor_copy(w_v[0][:, :, :], ek[:, 1, :, :]).then_inc(v_split, 1)
                            pool.wait_ge(v_split, 1)
                            pool.tensor_tensor(w_v[1][:, :, :], ek[:, 1, :, :], w_v[0][:, :, :],
                                               ALU.subtract).then_inc(v_split, 1)

                    for b in range(BATCH):
                        for number in (KEYS, VALUES, OUTPUT):
                            pass_loop(pair, b, number)(pool)

                @block.scalar
                def _(act):
                    gc_scalar(act)

                    def normalize(b, u, q, tiles):
                        wait(act, xg_used, q - 1)
                        for ct in tiles:
                            k = CT * b + ct
                            wait(act, lowered, CT * q + ct - 1)
                            for target in (xg[:, ct % 2, :], xg_parts[0][:, u, ct, :]):
                                normal = act.activation(target, xl[:, u, ct, :], ACT.Identity,
                                                        scale=gn1_scale[:, k:k + 1], bias=gn1_bias[:, k:k + 1])
                            normal.then_inc(normed, 1)

                    def exponentials(u, cb, a, m):
                        if m == 0:
                            wait(act, tr_mm, CT * (a - 1))
                            settle(act, act_fence)
                        act.activation(ek[:, u, m, :], keys[:, m, bass.ds(cb * T, T)], ACT.Exp,
                                       bias=neg_max[:, m:m + 1],
                                       accum_out=key_sum[:, m, bass.ds(cb, 1)]).then_inc(exp_done, 1)

                    act.wait_ge(w1_loaded, 16)
                    act.activation(w_k[0][:, :, :], ek[:, 0, :, :], ACT.Copy).then_inc(k_high, 1)
                    act.wait_ge(gn1_done, 1)
                    act.wait_ge(loaded[0], 16)
                    normalize(0, 0, 0, range(CT))

                    def pair(act, b, number, i):
                        for u in range(2):
                            a, q = CB * b + 2 * i + u, 3 * CB * b + CB * number + 2 * i + u
                            cb = 2 * i + u
                            same = not (isinstance(i, int) and i == PAIRS - 1 and u == 1)
                            nb = b if same else b + (number == OUTPUT)
                            half = 3 * PAIRS * b + PAIRS * number + i + u
                            if nb < BATCH:
                                act.wait_ge(loaded[1 - u], 16 * (half + 1))
                                if number != VALUES:
                                    normalize(nb, 1 - u, q + 1, range(CT))
                            if number == KEYS:
                                for m in range(CT):
                                    act.wait_ge(k_mm, CT * a + m + 1)
                                    settle(act, act_fence)
                                    act.activation(keys[:, m, bass.ds(cb * T, T)], banks[m][:, :],
                                                   ACT.Copy).then_inc(k_copied, 1)
                            if number == VALUES:
                                for lb in range(CT):
                                    if same:
                                        exponentials(1 - u, cb + 1, a + 1, lb)
                                    normalize(nb, 1 - u, q + 1, (lb,))
                                    block_no = CT * a + lb
                                    act.wait_ge(v_mm, block_no + 1)
                                    wait(act, ctx_mm, block_no - 1)
                                    act.activation(v_t[:, lb % 2, :], banks[lb % 2][:, :],
                                                   ACT.Copy).then_inc(v_copied, 1)

                    for b in range(BATCH):
                        for u in range(2):
                            wait(act, stored[u], 16 * PAIRS * b)
                        pass_loop(pair, b, KEYS)(act)
                        act.wait_ge(k_copied, CT * CB * (b + 1))
                        act.wait_ge(max_ready, b + 1)
                        act.wait_ge(k_split, 1)
                        act.wait_ge(v_split, 2)
                        for m in range(CT):
                            exponentials(0, 0, CB * b, m)
                        pass_loop(pair, b, VALUES)(act)
                        wait(act, y_mm, CT * CB * b)
                        for ct in range(CT):
                            act.wait_ge(m_mm, CT * b + ct + 1)
                            act.activation(m_sb[0][:, ct, :], banks[ct][:, :], ACT.Copy).then_inc(m_high, 1)
                        pass_loop(pair, b, OUTPUT)(act)

                @block.vector
                def _(dve):
                    gc_vector(dve, gn1_done)
                    dve.wait_ge(k_high, 1)
                    dve.tensor_tensor(w_k[1][:, :, :], ek[:, 0, :, :], w_k[0][:, :, :], ALU.subtract).then_inc(k_split, 1)
                    dve.wait_ge(zeroed, 1)

                    def pair(dve, b, number, i):
                        for u in range(2):
                            a = CB * b + 2 * i + u
                            cb = 2 * i + u
                            if number == KEYS:
                                for m in range(CT):
                                    dve.wait_ge(k_copied, CT * a + m + 1)
                                    settle(dve, dve_fence)
                                    dve.tensor_reduce(key_max[:, m, bass.ds(cb, 1)],
                                                      keys[:, m, bass.ds(cb * T, T)], AX.X,
                                                      ALU.max).then_inc(k_maxed, 1)
                            if number == VALUES:
                                for lb in range(CT):
                                    block_no = CT * a + lb
                                    dve.wait_ge(tr_mm, block_no + 1)
                                    wait(dve, ctx_mm, block_no - 1)
                                    dve.tensor_copy(ek_t[:, lb % 2, :], banks[2 + lb % 2][:, :]).then_inc(ek_copied, 1)
                            if number == OUTPUT:
                                wait(dve, stored[u], 16 * (PAIRS * b + i))
                                for o in range(CT):
                                    dve.wait_ge(y_mm, CT * a + o + 1)
                                    dve.scalar_tensor_tensor(y_out(u)[:, o, :], banks[o][:, :], b_o[:, o:o + 1],
                                                             xl[:, u, o, :], ALU.add, ALU.add).then_inc(y_ready, 1)

                    for b in range(BATCH):
                        pass_loop(pair, b, KEYS)(dve)
                        dve.wait_ge(k_maxed, CT * CB * (b + 1))
                        dve.tensor_reduce(neg_max[:, :], key_max[:, :, :], AX.X, ALU.max).then_inc(max_step, 1)
                        dve.wait_ge(max_step, b + 1)
                        dve.tensor_scalar(neg_max[:, :], neg_max[:, :], -1.0, None, ALU.mult).then_inc(max_ready, 1)
                        pass_loop(pair, b, VALUES)(dve)
                        dve.wait_ge(exp_done, CT * CB * (b + 1))
                        dve.tensor_reduce(inv_sum[:, :], key_sum[:, :, :], AX.X, ALU.add).then_inc(sum_step, 1)
                        dve.wait_ge(sum_step, 2 * b + 1)
                        dve.reciprocal(inv_sum[:, :], inv_sum[:, :]).then_inc(sum_step, 1)
                        dve.wait_ge(ctx_mm, CT * CB * (b + 1))
                        for m in range(CT):
                            for lo in (0, 64):
                                dve.tensor_copy(context[lo:lo + 64, m, lo:lo + 64],
                                                banks[4 + m][lo:lo + 64, lo:lo + 64]).then_inc(ctx_copied, 1)
                        dve.wait_ge(sum_step, 2 * b + 2)
                        wait(dve, m_mm, CT * b)
                        for m in range(CT):
                            dve.wait_ge(g_mm, CT * b + m + 1)
                            dve.tensor_scalar(g_sb[:, m, :], banks[m][:, :], inv_sum[:, m:m + 1], None,
                                              ALU.mult).then_inc(g_ready, 1)
                        for ct in range(CT):
                            dve.wait_ge(m_high, CT * b + ct + 1)
                            dve.tensor_tensor(m_sb[1][:, ct, :], banks[ct][:, :], m_sb[0][:, ct, :],
                                              ALU.subtract).then_inc(m_ready, 1)
                        dve.wait_ge(w1_rest_loaded, 64)
                        pass_loop(pair, b, OUTPUT)(dve)

                @block.tensor
                def _(pe):
                    gc_tensor(pe)
                    pe.wait_ge(k_split, 1)
                    pe.wait_ge(gn1_done, 1)

                    def context_products(block_no, lb, start, stop):
                        pe.wait_ge(v_copied, block_no + 1)
                        pe.wait_ge(ek_copied, block_no + 1)
                        for m in range(CT):
                            mm = pe.matmul(banks[4 + m][:, 0:P], v_t[:, lb % 2, m * P:(m + 1) * P],
                                           ek_t[:, lb % 2, m * P:(m + 1) * P], start=start, stop=stop)
                        mm.then_inc(ctx_mm, 1)

                    def pair(pe, b, number, i):
                        for u in range(2):
                            a, q = CB * b + 2 * i + u, 3 * CB * b + CB * number + 2 * i + u
                            pe.wait_ge(lowered, CT * (q + 1))
                            if number == KEYS:
                                for m in range(CT):
                                    wait(pe, k_copied, CT * (a - 1) + m + 1)
                                    products(pe, banks[m][:, :],
                                             lambda part, ct: w_k[part][:, ct, m * P:(m + 1) * P],
                                             lambda part, ct: xg_parts[part][:, u, ct, :]).then_inc(k_mm, 1)
                                pe.wait_ge(k_mm, CT * (a + 1))
                                pe.sem_inc(xg_used, 1)
                            if number == VALUES:
                                for lb in range(CT):
                                    block_no = CT * a + lb
                                    wait(pe, v_copied, block_no - 1)
                                    products(pe, banks[lb % 2][:, :],
                                             lambda part, ct: xg_parts[part][:, u, ct, lb * P:(lb + 1) * P],
                                             lambda part, ct: w_v[part][:, ct, :]).then_inc(v_mm, 1)
                                    if lb == 0:
                                        pe.wait_ge(exp_done, CT * (a + 1))
                                    wait(pe, ek_copied, block_no - 1)
                                    for m in range(CT):
                                        mm = pe.transpose(banks[2 + lb % 2][:, m * P:(m + 1) * P],
                                                          ek[:, u, m, lb * P:(lb + 1) * P], identity[:, :])
                                    mm.then_inc(tr_mm, 1)
                                    first = isinstance(i, int) and i == 0 and u == 0
                                    if not (first and lb == 0):
                                        context_products(block_no - 1, lb - 1, first and lb == 1, False)
                                pe.wait_ge(tr_mm, CT * (a + 1))
                                pe.sem_inc(xg_used, 1)
                            if number == OUTPUT:
                                for o in range(CT):
                                    wait(pe, y_ready, CT * (a - 1) + o + 1)
                                    products(pe, banks[o][:, :],
                                             lambda part, ct: m_sb[part][:, ct, o * P:(o + 1) * P],
                                             lambda part, ct: xg_parts[part][:, u, ct, :]).then_inc(y_mm, 1)
                                pe.wait_ge(y_mm, CT * (a + 1))
                                pe.sem_inc(xg_used, 1)

                    for b in range(BATCH):
                        wait(pe, y_ready, CT * CB * b)
                        pass_loop(pair, b, KEYS)(pe)
                        pe.wait_ge(k_copied, CT * CB * (b + 1))
                        pe.wait_ge(w1_rest_loaded, 64)
                        pe.wait_ge(v_split, 2)
                        wait(pe, ctx_copied, 2 * CT * b)
                        pass_loop(pair, b, VALUES)(pe)
                        context_products(CT * CB * (b + 1) - 1, CT - 1, False, True)
                        for m in range(CT):
                            pe.wait_ge(ctx_copied, 2 * CT * b + 2 * m + 2)
                            pe.matmul(banks[m][:, :], context[:, m, :], w_o[:, m, :], start=True,
                                      stop=True).then_inc(g_mm, 1)
                        pe.wait_ge(g_ready, CT * (b + 1))
                        for ct in range(CT):
                            for m in range(CT):
                                mm = pe.matmul(banks[ct][:, :], w_q[:, m, ct * P:(ct + 1) * P], g_sb[:, m, :],
                                               start=m == 0, stop=m == CT - 1)
                            mm.then_inc(m_mm, 1)
                        pe.wait_ge(m_ready, CT * (b + 1))
                        pass_loop(pair, b, OUTPUT)(pe)


def kernel(**inputs):
    import numpy as _np
    import concourse.bacc as _bacc
    from concourse import mybir as _mybir
    from concourse.bass_utils import run_bass_kernel_spmd as _run

    def rows(v, k):
        v = _np.asarray(v)
        return _np.ascontiguousarray(_np.moveaxis(v.reshape((k, 128) + v.shape[1:]), 0, 1))

    g = {k: _np.asarray(v) for k, v in inputs.items()}
    laid = {
        "x": g["x"].reshape(2, 512, 4096),
        "ln_w": rows(g["L0_conv_ln_w"], 4),
        "ln_b": rows(g["L0_conv_ln_b"], 4),
        "in_proj": g["L0_conv_in_proj_w"].T,
        "conv_w": rows(g["L0_conv_conv_w"], 8),
        "conv_b": rows(g["L0_conv_conv_b"], 8),
        "x_proj": g["L0_conv_x_proj_w"][[*range(32)] * 3 + [*range(32, 64)]].T,
        "dt_proj": _np.concatenate([g["L0_conv_dt_proj_w"].T] * 3),
        "dt_b": rows(g["L0_conv_dt_proj_b"], 8),
        "a_log": rows(g["L0_conv_A_log"], 8),
        "d_skip": rows(g["L0_conv_D_skip"], 8),
        "out_proj": g["L0_conv_out_proj_w"].T,
        "qkv": g["L1_conv_w_qkv"].T,
        "q_rows": g["L1_conv_w_qkv"][:512],
        "w_out1": g["L1_conv_w_out"].T,
        "b_out1": rows(g["L1_conv_b_out"], 4),
    }
    nc = _bacc.Bacc("TRN2", target_bir_lowering=False, num_devices=1, dynamic_dma_scratch_size=1024)
    arrays, args = {}, []
    for name, a in laid.items():
        a = _np.ascontiguousarray(a)
        arrays[f"in_{name}"] = a
        args.append(nc.dram_tensor(f"in_{name}", a.shape, _mybir.dt.from_np(a.dtype), kind="ExternalInput").ap())
    args.append(nc.dram_tensor("out_0", (2, 512, 4096), _mybir.dt.float32, kind="ExternalOutput").ap())
    mamba_and_linear_attention(nc, *args)
    r = _run(nc, [arrays], core_ids=[0])
    return r.results[0]["out_0"].reshape(2, 512, 64, 64)
```
